# Optimizing a Trainium2 kernel written in Bass

```python
import numpy as np
import jax
import jax.numpy as jnp

def _softmax(x, axis=-1):
    return jax.nn.softmax(x, axis=axis)

def _gelu(x):
    return jax.nn.gelu(x, approximate=True)

def _silu(x):
    return jax.nn.silu(x)

def _sigmoid(x):
    return jax.nn.sigmoid(x)

def _layernorm(x, axis=-1, eps=1e-05):
    m = jnp.mean(x, axis=axis, keepdims=True)
    v = jnp.var(x, axis=axis, keepdims=True)
    return (x - m) / jnp.sqrt(v + eps)

def _scatter_add(tgt, idx, src, axis=0):
    return tgt.at[idx].add(src)

def _segment_sum(src, seg, n):
    return jax.ops.segment_sum(src, seg, n)
kernel_name = 'mk_decoder_preln_d2_seqx_r4_f7aed9'

def setup_inputs(seed: int=0):
    np.random.seed(seed)
    _w = jnp.asarray

    def _rec_inputs():
        import jax
        import jax.numpy as jnp
        _rk = jax.random.key(seed)
        x = -0.0002928 + 1 * jax.random.normal(jax.random.fold_in(_rk, 1), (64, 128, 256), jnp.float32)
        _lenS = 128 - jax.random.randint(jax.random.fold_in(_rk, 7), (64,), 0, max(1, 128 // 4) + 1, jnp.int32)
        _lenS2 = 128 - jax.random.randint(jax.random.fold_in(_rk, 8), (64,), 0, max(1, 128 // 4) + 1, jnp.int32)
        _ctx_1024P = jax.random.normal(jax.random.fold_in(_rk, 11), (64, 16, 256), jnp.float32)
        _ctx_1024c = jax.random.dirichlet(jax.random.fold_in(_rk, 511), 0.3 * jnp.ones((16,), jnp.float32), (64, 128))
        _ctx_1024t = jnp.einsum('bsk,bkd->bsd', _ctx_1024c, _ctx_1024P)
        _ctx_1024t = _ctx_1024t * jax.lax.rsqrt(jnp.mean(jnp.square(_ctx_1024t)) + 1e-12) * 0.953939
        ctx_1024 = -1.39393e-06 + 0.999914 * (_ctx_1024t + 0.3 * jax.random.normal(jax.random.fold_in(_rk, 611), (64, 128, 256), jnp.float32))
        _validS = jnp.arange(128)[None, :] < _lenS[:, None]
        _validS2 = jnp.arange(128)[None, :] < _lenS2[:, None]
        _causal = jnp.tril(jnp.ones((128, 128), dtype=bool))
        mask_BxS2_fk1 = jnp.where(jnp.broadcast_to(_validS2[:, :], (64, 128)), 1.0, 0.0).astype(jnp.float32)
        return (x, ctx_1024, mask_BxS2_fk1)
    x, ctx_1024, mask_BxS2_fk1 = _rec_inputs()

    def _L0_attn_setup():
        import jax, jax.numpy as jnp
        import numpy as np
        D_MODEL = 256
        H = 16
        DH = D_MODEL // H
        WIN = 7
        PAD = WIN // 2
        B, L = (2, 1024)
        key = jax.random.key(seed)
        ks = jax.random.split(key, 12)
        s = lambda k, shape: jax.random.normal(k, shape, dtype=jnp.float32) * 0.02
        return {'x': jax.random.normal(ks[0], (B, L, D_MODEL), dtype=jnp.float32), 'wq': s(ks[1], (D_MODEL, D_MODEL)), 'wk': s(ks[2], (D_MODEL, D_MODEL)), 'wv': s(ks[3], (D_MODEL, D_MODEL)), 'wo': s(ks[4], (D_MODEL, D_MODEL)), 'bo': s(ks[5], (D_MODEL,)), 'cw1': s(ks[6], (H, 32, 1)), 'cb1': s(ks[7], (H, 32)), 'cw2': s(ks[8], (H, 32, 32)), 'cb2': s(ks[9], (H, 32)), 'cw3': s(ks[10], (H, 1, 32)), 'cb3': s(ks[11], (H, 1))}
    _L0_attn_all = _L0_attn_setup()
    _L0_attn_in = {k: v for k, v in _L0_attn_all.items() if k in ('wq', 'wk', 'wv', 'wo', 'bo', 'cw1', 'cb1', 'cw2', 'cb2', 'cw3', 'cb3')}
    del _L0_attn_all

    def _L0_xattn_setup():
        import jax, jax.numpy as jnp
        import numpy as np
        B, S, D, H = (2, 512, 256, 16)
        DK = D // H
        OUT = 256
        key = jax.random.key(seed)
        kq, kk, kv, kl, kw, kb = jax.random.split(key, 6)
        query = jax.random.normal(kq, (B, S, D), dtype=jnp.float32)
        k_ = jax.random.normal(kk, (B, S, D), dtype=jnp.float32)
        v_ = jax.random.normal(kv, (B, S, D), dtype=jnp.float32)
        lengths = jax.random.randint(kl, (B,), S // 2, S + 1)
        mask = (jnp.arange(S)[None, :] < lengths[:, None]).astype(jnp.float32)
        bound = 1.0 / np.sqrt(D)
        Wp = jax.random.uniform(kw, (OUT, D), minval=-bound, maxval=bound, dtype=jnp.float32)
        bp = jax.random.uniform(kb, (OUT,), minval=-bound, maxval=bound, dtype=jnp.float32)
        return {'query': query, 'key': k_, 'value': v_, 'mask': mask, 'Wp': Wp, 'bp': bp}
    _L0_xattn_all = _L0_xattn_setup()
    _L0_xattn_in = {k: v for k, v in _L0_xattn_all.items() if k in ('Wp', 'bp')}
    del _L0_xattn_all

    def _L0_ffn_setup():
        import jax, jax.numpy as jnp
        import numpy as np
        D_MODEL = 256
        NUM_SLOTS = 64
        TOP_K = 8
        B, T = (4, 1024)

        def _forward(x, slot_init, slot_scale, w1, b1, w2, b2, gru_wih, gru_whh, gru_bih, gru_bhh, wv, bv, wo, bo, tau):
            Bn, Tn, D = x.shape
            Sn = slot_init.shape[0]
            S = jnp.broadcast_to((slot_init * slot_scale)[None], (Bn, Sn, D)).astype(x.dtype)
            slot_mean = S.mean(axis=1, keepdims=True)
            ctx = jnp.concatenate([x, jnp.broadcast_to(slot_mean, x.shape)], axis=-1)
            h = jax.nn.gelu(ctx @ w1.T + b1, approximate=False)
            route_logits = (h @ w2.T + b2) / (jnp.abs(tau) + 0.1)
            topk_vals, topk_idx = jax.lax.top_k(route_logits, TOP_K)
            topk_w = jax.nn.softmax(topk_vals, axis=-1)
            alpha = jnp.sum(topk_w[..., None] * jax.nn.one_hot(topk_idx, Sn, dtype=x.dtype), axis=-2)
            slot_input = jnp.einsum('bts,btd->bsd', alpha, x)
            slot_wsum = alpha.sum(axis=1) + 1e-08
            gi = (slot_input / slot_wsum[..., None]).reshape(Bn * Sn, D)
            hs = S.reshape(Bn * Sn, D)
            gx = gi @ gru_wih.T + gru_bih
            gh = hs @ gru_whh.T + gru_bhh
            xr, xz, xn = jnp.split(gx, 3, axis=-1)
            hr, hz, hn = jnp.split(gh, 3, axis=-1)
            r = jax.nn.sigmoid(xr + hr)
            z = jax.nn.sigmoid(xz + hz)
            n = jnp.tanh(xn + r * hn)
            h_new = (1.0 - z) * n + z * hs
            S_new = h_new.reshape(Bn, Sn, D)
            slot_values = S_new @ wv.T + bv
            out = jnp.einsum('bts,bsd->btd', alpha, slot_values)
            return out @ wo.T + bo
        key = jax.random.key(seed)
        ks = jax.random.split(key, 16)
        D, S = (D_MODEL, NUM_SLOTS)
        H = D // 2
        sc = lambda fan_in: 1.0 / np.sqrt(fan_in)
        inp = {'x': jax.random.normal(ks[0], (B, T, D), dtype=jnp.float32), 'slot_init': jax.random.normal(ks[1], (S, D), dtype=jnp.float32) * 0.1, 'slot_scale': jnp.ones((S, 1), dtype=jnp.float32), 'w1': jax.random.normal(ks[2], (H, 2 * D), dtype=jnp.float32) * sc(2 * D), 'b1': jnp.zeros((H,), dtype=jnp.float32), 'w2': jax.random.normal(ks[3], (S, H), dtype=jnp.float32) * sc(H), 'b2': jnp.zeros((S,), dtype=jnp.float32), 'gru_wih': jax.random.normal(ks[4], (3 * D, D), dtype=jnp.float32) * sc(D), 'gru_whh': jax.random.normal(ks[5], (3 * D, D), dtype=jnp.float32) * sc(D), 'gru_bih': jnp.zeros((3 * D,), dtype=jnp.float32), 'gru_bhh': jnp.zeros((3 * D,), dtype=jnp.float32), 'wv': jax.random.normal(ks[6], (D, D), dtype=jnp.float32) * sc(D), 'bv': jnp.zeros((D,), dtype=jnp.float32), 'wo': jax.random.normal(ks[7], (D, D), dtype=jnp.float32) * sc(D), 'bo': jnp.zeros((D,), dtype=jnp.float32), 'tau': jnp.ones((1,), dtype=jnp.float32)}
        return inp
    _L0_ffn_all = _L0_ffn_setup()
    _L0_ffn_in = {k: v for k, v in _L0_ffn_all.items() if k in ('slot_init', 'slot_scale', 'w1', 'b1', 'w2', 'b2', 'gru_wih', 'gru_whh', 'gru_bih', 'gru_bhh', 'wv', 'bv', 'wo', 'bo', 'tau')}
    del _L0_ffn_all

    def _L1_attn_setup():
        import jax, jax.numpy as jnp
        import numpy as np
        INIT_L = 512.0
        EPS = 1e-06
        N_HEAD = 16

        def fire_bias(T, w1, b1, w2, b2, c, L_multiplier):
            pos = jnp.arange(T, dtype=jnp.float32)
            rel = pos[:, None] - pos[None, :]
            threshold = jnp.abs(L_multiplier * INIT_L)
            pos_norm = jnp.maximum(pos, threshold)[:, None]
            rel = jnp.log(jnp.abs(c * rel) + 1.0)
            pos_norm = jnp.log(jnp.abs(c * pos_norm) + 1.0) + EPS
            nd = rel / pos_norm
            h = jax.nn.relu(nd[..., None] * w1[0] + b1)
            bias = jnp.einsum('tsw,wh->hts', h, w2) + b2[:, None, None]
            causal = jnp.tril(jnp.ones((T, T), dtype=bool))
            bias = jnp.where(causal[None], bias, -jnp.inf)
            return bias[None]
        key = jax.random.key(seed)
        ks = jax.random.split(key, 8)
        B, T, C, H, W = (2, 512, 256, 16, 32)
        s = 0.02
        return {'x': jax.random.normal(ks[0], (B, T, C), jnp.float32), 'Wqkv': jax.random.normal(ks[1], (C, 3 * C), jnp.float32) * s, 'bqkv': jnp.zeros((3 * C,), jnp.float32), 'Wproj': jax.random.normal(ks[2], (C, C), jnp.float32) * s, 'bproj': jnp.zeros((C,), jnp.float32), 'w1': jax.random.normal(ks[3], (1, W), jnp.float32), 'b1': jnp.zeros((W,), jnp.float32), 'w2': jax.random.normal(ks[4], (W, H), jnp.float32) * 0.1, 'b2': jnp.zeros((H,), jnp.float32), 'c_param': jnp.float32(0.1), 'L_multiplier': jnp.float32(1.0)}
    _L1_attn_all = _L1_attn_setup()
    _L1_attn_in = {k: v for k, v in _L1_attn_all.items() if k in ('Wqkv', 'bqkv', 'Wproj', 'bproj', 'w1', 'b1', 'w2', 'b2', 'c_param', 'L_multiplier')}
    del _L1_attn_all

    def _L1_xattn_setup():
        import jax, jax.numpy as jnp
        import numpy as np
        HIDDEN = 256
        NUM_HEADS = 16
        HEAD_DIM = HIDDEN // NUM_HEADS
        SCALE = 1.0 / float(np.sqrt(HEAD_DIM))
        key = jax.random.key(seed)
        ks = jax.random.split(key, 10)
        B, SQ, SKV = (2, 512, 1024)
        init = 0.02
        return {'query_states': jax.random.normal(ks[0], (B, SQ, HIDDEN), dtype=jnp.float32), 'key_value_states': jax.random.normal(ks[1], (B, SKV, HIDDEN), dtype=jnp.float32), 'Wq': jax.random.normal(ks[2], (HIDDEN, HIDDEN), dtype=jnp.float32) * init, 'bq': jnp.zeros((HIDDEN,), dtype=jnp.float32), 'Wk': jax.random.normal(ks[3], (HIDDEN, HIDDEN), dtype=jnp.float32) * init, 'bk': jnp.zeros((HIDDEN,), dtype=jnp.float32), 'Wv': jax.random.normal(ks[4], (HIDDEN, HIDDEN), dtype=jnp.float32) * init, 'bv': jnp.zeros((HIDDEN,), dtype=jnp.float32), 'Wo': jax.random.normal(ks[5], (HIDDEN, HIDDEN), dtype=jnp.float32) * init, 'bo': jnp.zeros((HIDDEN,), dtype=jnp.float32)}
    _L1_xattn_all = _L1_xattn_setup()
    _L1_xattn_in = {k: v for k, v in _L1_xattn_all.items() if k in ('Wq', 'bq', 'Wk', 'bk', 'Wv', 'bv', 'Wo', 'bo')}
    del _L1_xattn_all

    def _L1_ffn_setup():
        import jax, jax.numpy as jnp
        import numpy as np
        B, S, D_MODEL, D_HIDDEN = (4, 512, 256, 1024)

        def act_quant(x):
            scale = 127.0 / jnp.clip(jnp.max(jnp.abs(x), axis=-1, keepdims=True), 1e-05)
            return jnp.clip(jnp.round(x * scale), -128, 127) / scale

        def weight_quant(w):
            scale = 1.0 / jnp.clip(jnp.mean(jnp.abs(w)), 1e-05)
            return jnp.clip(jnp.round(w * scale), -1, 1) / scale

        def bit_linear(x, w):
            xq = x + jax.lax.stop_gradient(act_quant(x) - x)
            wq = w + jax.lax.stop_gradient(weight_quant(w) - w)
            return jnp.einsum('bsd,hd->bsh', xq, wq)

        def depthwise_conv1d(x_bcl, w, b):
            y = jax.lax.conv_general_dilated(x_bcl, w, window_strides=(1,), padding=[(1, 1)], dimension_numbers=('NCH', 'OIH', 'NCH'), feature_group_count=x_bcl.shape[1])
            return y + b[None, :, None]
        key = jax.random.key(seed)
        ks = jax.random.split(key, 5)
        lim1 = 1.0 / np.sqrt(D_MODEL)
        lim2 = 1.0 / np.sqrt(D_HIDDEN)
        limc = 1.0 / np.sqrt(3.0)
        return {'x': jax.random.normal(ks[0], (B, S, D_MODEL), dtype=jnp.float32), 'w1': jax.random.uniform(ks[1], (D_HIDDEN, D_MODEL), jnp.float32, -lim1, lim1), 'conv_w': jax.random.uniform(ks[2], (D_HIDDEN, 1, 3), jnp.float32, -limc, limc), 'conv_b': jax.random.uniform(ks[3], (D_HIDDEN,), jnp.float32, -limc, limc), 'w2': jax.random.uniform(ks[4], (D_MODEL, D_HIDDEN), jnp.float32, -lim2, lim2)}
    _L1_ffn_all = _L1_ffn_setup()
    _L1_ffn_in = {k: v for k, v in _L1_ffn_all.items() if k in ('w1', 'conv_w', 'conv_b', 'w2')}
    del _L1_ffn_all
    return {'x': x, 'ctx_1024': ctx_1024, 'mask_BxS2_fk1': mask_BxS2_fk1, 'L0_attn_wq': _L0_attn_in['wq'], 'L0_attn_wk': _L0_attn_in['wk'], 'L0_attn_wv': _L0_attn_in['wv'], 'L0_attn_wo': _L0_attn_in['wo'], 'L0_attn_bo': _L0_attn_in['bo'], 'L0_attn_cw1': _L0_attn_in['cw1'], 'L0_attn_cb1': _L0_attn_in['cb1'], 'L0_attn_cw2': _L0_attn_in['cw2'], 'L0_attn_cb2': _L0_attn_in['cb2'], 'L0_attn_cw3': _L0_attn_in['cw3'], 'L0_attn_cb3': _L0_attn_in['cb3'], 'L0_xattn_Wp': _L0_xattn_in['Wp'], 'L0_xattn_bp': _L0_xattn_in['bp'], 'L0_ffn_slot_init': _L0_ffn_in['slot_init'], 'L0_ffn_slot_scale': _L0_ffn_in['slot_scale'], 'L0_ffn_w1': _L0_ffn_in['w1'], 'L0_ffn_b1': _L0_ffn_in['b1'], 'L0_ffn_w2': _L0_ffn_in['w2'], 'L0_ffn_b2': _L0_ffn_in['b2'], 'L0_ffn_gru_wih': _L0_ffn_in['gru_wih'], 'L0_ffn_gru_whh': _L0_ffn_in['gru_whh'], 'L0_ffn_gru_bih': _L0_ffn_in['gru_bih'], 'L0_ffn_gru_bhh': _L0_ffn_in['gru_bhh'], 'L0_ffn_wv': _L0_ffn_in['wv'], 'L0_ffn_bv': _L0_ffn_in['bv'], 'L0_ffn_wo': _L0_ffn_in['wo'], 'L0_ffn_bo': _L0_ffn_in['bo'], 'L0_ffn_tau': _L0_ffn_in['tau'], 'L1_attn_Wqkv': _L1_attn_in['Wqkv'], 'L1_attn_bqkv': _L1_attn_in['bqkv'], 'L1_attn_Wproj': _L1_attn_in['Wproj'], 'L1_attn_bproj': _L1_attn_in['bproj'], 'L1_attn_w1': _L1_attn_in['w1'], 'L1_attn_b1': _L1_attn_in['b1'], 'L1_attn_w2': _L1_attn_in['w2'], 'L1_attn_b2': _L1_attn_in['b2'], 'L1_attn_c_param': _L1_attn_in['c_param'], 'L1_attn_L_multiplier': _L1_attn_in['L_multiplier'], 'L1_xattn_Wq': _L1_xattn_in['Wq'], 'L1_xattn_bq': _L1_xattn_in['bq'], 'L1_xattn_Wk': _L1_xattn_in['Wk'], 'L1_xattn_bk': _L1_xattn_in['bk'], 'L1_xattn_Wv': _L1_xattn_in['Wv'], 'L1_xattn_bv': _L1_xattn_in['bv'], 'L1_xattn_Wo': _L1_xattn_in['Wo'], 'L1_xattn_bo': _L1_xattn_in['bo'], 'L1_ffn_w1': _L1_ffn_in['w1'], 'L1_ffn_conv_w': _L1_ffn_in['conv_w'], 'L1_ffn_conv_b': _L1_ffn_in['conv_b'], 'L1_ffn_w2': _L1_ffn_in['w2']}

def reference(x, ctx_1024, mask_BxS2_fk1, L0_attn_wq, L0_attn_wk, L0_attn_wv, L0_attn_wo, L0_attn_bo, L0_attn_cw1, L0_attn_cb1, L0_attn_cw2, L0_attn_cb2, L0_attn_cw3, L0_attn_cb3, L0_xattn_Wp, L0_xattn_bp, L0_ffn_slot_init, L0_ffn_slot_scale, L0_ffn_w1, L0_ffn_b1, L0_ffn_w2, L0_ffn_b2, L0_ffn_gru_wih, L0_ffn_gru_whh, L0_ffn_gru_bih, L0_ffn_gru_bhh, L0_ffn_wv, L0_ffn_bv, L0_ffn_wo, L0_ffn_bo, L0_ffn_tau, L1_attn_Wqkv, L1_attn_bqkv, L1_attn_Wproj, L1_attn_bproj, L1_attn_w1, L1_attn_b1, L1_attn_w2, L1_attn_b2, L1_attn_c_param, L1_attn_L_multiplier, L1_xattn_Wq, L1_xattn_bq, L1_xattn_Wk, L1_xattn_bk, L1_xattn_Wv, L1_xattn_bv, L1_xattn_Wo, L1_xattn_bo, L1_ffn_w1, L1_ffn_conv_w, L1_ffn_conv_b, L1_ffn_w2):
    import jax
    import jax.numpy as jnp

    def _L0_attn_ref(x, wq, wk, wv, wo, bo, cw1, cb1, cw2, cb2, cw3, cb3):
        import jax, jax.numpy as jnp
        import numpy as np
        D_MODEL = 256
        H = 16
        DH = D_MODEL // H
        WIN = 7
        PAD = WIN // 2
        B, L = (2, 1024)
        b, l, d = x.shape

        def heads(w):
            return (x @ w.T).reshape(b, l, H, DH).transpose(0, 2, 1, 3)
        Q, K, V = (heads(wq), heads(wk), heads(wv))
        Kp = jnp.pad(K, ((0, 0), (0, 0), (PAD, PAD), (0, 0)))
        Vp = jnp.pad(V, ((0, 0), (0, 0), (PAD, PAD), (0, 0)))
        idx = jnp.arange(l)[:, None] + jnp.arange(WIN)[None, :]
        Kw = Kp[:, :, idx]
        Vw = Vp[:, :, idx]
        scores = jnp.einsum('bhld,bhlwd->bhlw', Q, Kw) / np.float32(np.sqrt(DH))
        attn = jax.nn.softmax(scores, axis=-1)
        pos = jnp.linspace(0.0, 1.0, WIN, dtype=jnp.float32)[:, None]
        gelu = lambda z: jax.nn.gelu(z, approximate=False)
        h = gelu(jnp.einsum('wi,hji->hwj', pos, cw1) + cb1[:, None, :])
        h = gelu(jnp.einsum('hwi,hji->hwj', h, cw2) + cb2[:, None, :])
        cwt = (jnp.einsum('hwi,hji->hwj', h, cw3) + cb3[:, None, :])[..., 0]
        conn = jax.nn.softmax(cwt, axis=-1)[None, :, None, :]
        fw = attn * conn
        fw = fw / (fw.sum(axis=-1, keepdims=True) + 1e-09)
        out = jnp.einsum('bhlw,bhlwd->bhld', fw, Vw)
        out = out.transpose(0, 2, 1, 3).reshape(b, l, d)
        return out @ wo.T + bo

    def _L0_xattn_ref(query, key, value, mask, Wp, bp):
        import jax, jax.numpy as jnp
        import numpy as np
        B, S, D, H = (2, 512, 256, 16)
        DK = D // H
        OUT = 256
        Bsz, Seq, Dm = query.shape
        score_mask = mask[:, :, None] * mask[:, None, :]
        q = query.reshape(Bsz, Seq, H, DK).transpose(0, 2, 1, 3)
        k = key.reshape(Bsz, Seq, H, DK).transpose(0, 2, 1, 3)
        v = value.reshape(Bsz, Seq, H, DK).transpose(0, 2, 1, 3)
        score = jnp.einsum('bhqd,bhkd->bhqk', q, k) / jnp.sqrt(jnp.float32(DK))
        sm = score_mask[:, None, :, :]
        score = jnp.where(sm == 0, jnp.float32(-1000000000.0), score)
        p_attn = jax.nn.softmax(score, axis=-1) * sm
        x = jnp.einsum('bhqk,bhkd->bhqd', p_attn, v)
        x = x.transpose(0, 2, 1, 3).reshape(Bsz, Seq, Dm)
        out = (x @ Wp.T + bp) * mask[:, :, None]
        return out

    def _L0_ffn_ref(x, slot_init, slot_scale, w1, b1, w2, b2, gru_wih, gru_whh, gru_bih, gru_bhh, wv, bv, wo, bo, tau):
        import jax, jax.numpy as jnp
        import numpy as np
        D_MODEL = 256
        NUM_SLOTS = 64
        TOP_K = 8
        B, T = (4, 1024)

        def _forward(x, slot_init, slot_scale, w1, b1, w2, b2, gru_wih, gru_whh, gru_bih, gru_bhh, wv, bv, wo, bo, tau):
            Bn, Tn, D = x.shape
            Sn = slot_init.shape[0]
            S = jnp.broadcast_to((slot_init * slot_scale)[None], (Bn, Sn, D)).astype(x.dtype)
            slot_mean = S.mean(axis=1, keepdims=True)
            ctx = jnp.concatenate([x, jnp.broadcast_to(slot_mean, x.shape)], axis=-1)
            h = jax.nn.gelu(ctx @ w1.T + b1, approximate=False)
            route_logits = (h @ w2.T + b2) / (jnp.abs(tau) + 0.1)
            topk_vals, topk_idx = jax.lax.top_k(route_logits, TOP_K)
            topk_w = jax.nn.softmax(topk_vals, axis=-1)
            alpha = jnp.sum(topk_w[..., None] * jax.nn.one_hot(topk_idx, Sn, dtype=x.dtype), axis=-2)
            slot_input = jnp.einsum('bts,btd->bsd', alpha, x)
            slot_wsum = alpha.sum(axis=1) + 1e-08
            gi = (slot_input / slot_wsum[..., None]).reshape(Bn * Sn, D)
            hs = S.reshape(Bn * Sn, D)
            gx = gi @ gru_wih.T + gru_bih
            gh = hs @ gru_whh.T + gru_bhh
            xr, xz, xn = jnp.split(gx, 3, axis=-1)
            hr, hz, hn = jnp.split(gh, 3, axis=-1)
            r = jax.nn.sigmoid(xr + hr)
            z = jax.nn.sigmoid(xz + hz)
            n = jnp.tanh(xn + r * hn)
            h_new = (1.0 - z) * n + z * hs
            S_new = h_new.reshape(Bn, Sn, D)
            slot_values = S_new @ wv.T + bv
            out = jnp.einsum('bts,bsd->btd', alpha, slot_values)
            return out @ wo.T + bo
        return _forward(x, slot_init, slot_scale, w1, b1, w2, b2, gru_wih, gru_whh, gru_bih, gru_bhh, wv, bv, wo, bo, tau)

    def _L1_attn_ref(x, Wqkv, bqkv, Wproj, bproj, w1, b1, w2, b2, c_param, L_multiplier):
        import jax, jax.numpy as jnp
        import numpy as np
        INIT_L = 512.0
        EPS = 1e-06
        N_HEAD = 16

        def fire_bias(T, w1, b1, w2, b2, c, L_multiplier):
            pos = jnp.arange(T, dtype=jnp.float32)
            rel = pos[:, None] - pos[None, :]
            threshold = jnp.abs(L_multiplier * INIT_L)
            pos_norm = jnp.maximum(pos, threshold)[:, None]
            rel = jnp.log(jnp.abs(c * rel) + 1.0)
            pos_norm = jnp.log(jnp.abs(c * pos_norm) + 1.0) + EPS
            nd = rel / pos_norm
            h = jax.nn.relu(nd[..., None] * w1[0] + b1)
            bias = jnp.einsum('tsw,wh->hts', h, w2) + b2[:, None, None]
            causal = jnp.tril(jnp.ones((T, T), dtype=bool))
            bias = jnp.where(causal[None], bias, -jnp.inf)
            return bias[None]
        B, T, C = x.shape
        H = N_HEAD
        hd = C // H
        qkv = x @ Wqkv + bqkv
        q, k, v = jnp.split(qkv, 3, axis=-1)
        q = q.reshape(B, T, H, hd).transpose(0, 2, 1, 3)
        k = k.reshape(B, T, H, hd).transpose(0, 2, 1, 3)
        v = v.reshape(B, T, H, hd).transpose(0, 2, 1, 3)
        bias = fire_bias(T, w1, b1, w2, b2, c_param, L_multiplier)
        scale = 1.0 / jnp.sqrt(jnp.float32(hd))
        att = jnp.einsum('bhqd,bhkd->bhqk', q, k) * scale + bias
        att = jax.nn.softmax(att, axis=-1)
        y = jnp.einsum('bhqk,bhkd->bhqd', att, v)
        y = y.transpose(0, 2, 1, 3).reshape(B, T, C)
        return y @ Wproj + bproj

    def _L1_xattn_ref(query_states, key_value_states, Wq, bq, Wk, bk, Wv, bv, Wo, bo):
        import jax, jax.numpy as jnp
        import numpy as np
        HIDDEN = 256
        NUM_HEADS = 16
        HEAD_DIM = HIDDEN // NUM_HEADS
        SCALE = 1.0 / float(np.sqrt(HEAD_DIM))
        B, SQ, _ = query_states.shape
        _, SKV, _ = key_value_states.shape
        q = query_states @ Wq.T + bq
        k = key_value_states @ Wk.T + bk
        v = key_value_states @ Wv.T + bv
        q = q.reshape(B, SQ, NUM_HEADS, HEAD_DIM).transpose(0, 2, 1, 3) * SCALE
        k = k.reshape(B, SKV, NUM_HEADS, HEAD_DIM).transpose(0, 2, 1, 3)
        v = v.reshape(B, SKV, NUM_HEADS, HEAD_DIM).transpose(0, 2, 1, 3)
        scores = jnp.einsum('bhqd,bhkd->bhqk', q, k)
        attn = jax.nn.softmax(scores, axis=-1)
        ctx = jnp.einsum('bhqk,bhkd->bhqd', attn, v)
        ctx = ctx.transpose(0, 2, 1, 3).reshape(B, SQ, HIDDEN)
        return ctx @ Wo.T + bo

    def _L1_ffn_ref(x, w1, conv_w, conv_b, w2):
        import jax, jax.numpy as jnp
        import numpy as np
        B, S, D_MODEL, D_HIDDEN = (4, 512, 256, 1024)

        def act_quant(x):
            scale = 127.0 / jnp.clip(jnp.max(jnp.abs(x), axis=-1, keepdims=True), 1e-05)
            return jnp.clip(jnp.round(x * scale), -128, 127) / scale

        def weight_quant(w):
            scale = 1.0 / jnp.clip(jnp.mean(jnp.abs(w)), 1e-05)
            return jnp.clip(jnp.round(w * scale), -1, 1) / scale

        def bit_linear(x, w):
            xq = x + jax.lax.stop_gradient(act_quant(x) - x)
            wq = w + jax.lax.stop_gradient(weight_quant(w) - w)
            return jnp.einsum('bsd,hd->bsh', xq, wq)

        def depthwise_conv1d(x_bcl, w, b):
            y = jax.lax.conv_general_dilated(x_bcl, w, window_strides=(1,), padding=[(1, 1)], dimension_numbers=('NCH', 'OIH', 'NCH'), feature_group_count=x_bcl.shape[1])
            return y + b[None, :, None]
        h = bit_linear(x, w1)
        h = depthwise_conv1d(h.transpose(0, 2, 1), conv_w, conv_b)
        h = h.transpose(0, 2, 1)
        h = jax.nn.silu(h)
        return bit_linear(h, w2)
    x = x + _L0_attn_ref(_layernorm(x, axis=-1), L0_attn_wq, L0_attn_wk, L0_attn_wv, L0_attn_wo, L0_attn_bo, L0_attn_cw1, L0_attn_cb1, L0_attn_cw2, L0_attn_cb2, L0_attn_cw3, L0_attn_cb3)
    x = x + _L0_xattn_ref(_layernorm(x, axis=-1), ctx_1024, ctx_1024, mask_BxS2_fk1, L0_xattn_Wp, L0_xattn_bp)
    x = x + _L0_ffn_ref(_layernorm(x, axis=-1), L0_ffn_slot_init, L0_ffn_slot_scale, L0_ffn_w1, L0_ffn_b1, L0_ffn_w2, L0_ffn_b2, L0_ffn_gru_wih, L0_ffn_gru_whh, L0_ffn_gru_bih, L0_ffn_gru_bhh, L0_ffn_wv, L0_ffn_bv, L0_ffn_wo, L0_ffn_bo, L0_ffn_tau)
    x = x + _L1_attn_ref(_layernorm(x, axis=-1), L1_attn_Wqkv, L1_attn_bqkv, L1_attn_Wproj, L1_attn_bproj, L1_attn_w1, L1_attn_b1, L1_attn_w2, L1_attn_b2, L1_attn_c_param, L1_attn_L_multiplier)
    x = x + _L1_xattn_ref(_layernorm(x, axis=-1), ctx_1024, L1_xattn_Wq, L1_xattn_bq, L1_xattn_Wk, L1_xattn_bk, L1_xattn_Wv, L1_xattn_bv, L1_xattn_Wo, L1_xattn_bo)
    x = x + _L1_ffn_ref(_layernorm(x, axis=-1), L1_ffn_w1, L1_ffn_conv_w, L1_ffn_conv_b, L1_ffn_w2)
    return x

_drawn_inputs = setup_inputs


def setup_inputs(seed=0):
    import zlib

    import numpy as np

    out = dict(_drawn_inputs(seed))
    spreads = {'L0_ffn_slot_scale': (1.0, 0.6),
     'L0_ffn_b1': (0.0, 0.377),
     'L0_ffn_b2': (0.0, 0.325),
     'L0_ffn_gru_bih': (0.0, 0.1),
     'L0_ffn_gru_bhh': (0.0, 0.4),
     'L0_ffn_bv': (0.0, 0.1),
     'L0_ffn_bo': (0.0, 0.1),
     'L1_attn_bqkv': (0.0, 0.1),
     'L1_attn_bproj': (0.0, 0.1),
     'L1_attn_b1': (0.0, 2.0),
     'L1_attn_b2': (0.0, 2.0),
     'L1_xattn_bq': (0.0, 0.8),
     'L1_xattn_bk': (0.0, 2.0),
     'L1_xattn_bv': (0.0, 0.29),
     'L1_xattn_bo': (0.0, 0.1)}
    factors = {'L0_attn_wq': 8.0,
     'L0_attn_wk': 8.0,
     'L0_attn_cw1': 64.0,
     'L0_attn_cb1': 64.0,
     'L0_attn_cw2': 64.0,
     'L0_attn_cb2': 64.0,
     'L0_attn_cw3': 64.0,
     'L0_ffn_slot_init': 2.713,
     'L0_ffn_gru_whh': 6.465,
     'L1_attn_w1': 21.36,
     'L1_attn_w2': 8.0,
     'L1_xattn_Wq': 8.0,
     'L1_xattn_Wk': 8.0,
     'L0_attn_cb3': 64.0}
    for name, (base, spread) in spreads.items():
        noise = np.random.default_rng([zlib.crc32(name.encode()), seed]).standard_normal(out[name].shape)
        drawn = base * np.exp(spread * noise) if base else spread * noise
        out[name] = jnp.asarray(drawn.astype(out[name].dtype))
    for name, factor in factors.items():
        out[name] = (out[name] * factor).astype(out[name].dtype)
    return out
```

```python
from contextlib import ExitStack

import numpy as np
import concourse.bass as bass
from concourse import mybir

F32 = mybir.dt.float32
BF16 = mybir.dt.bfloat16
ACT = mybir.ActivationFunctionType
ALU = mybir.AluOpType
AX = mybir.AxisListType

NSEQ, T, D = 64, 128, 256
H, DH = 16, 16
KT = D // 128
WIN, PAD = 7, 3
SLOTS, GATES = 64, 768
HID = 1024
HT = HID // 128
NCHAIN = 2
TURNS = NSEQ // NCHAIN
LN_EPS = 1e-5
ROUND = 12582912.0
MASKED = 1e9
CAUSAL = 1e30
GROUPS = 4
PER = H // GROUPS
VC = DH + 1

PE, DVE, ACTE, POOL, SP = "tensor", "vector", "scalar", "gpsimd", "sync"


class Step:
    def __init__(self, engine, name, emit, after, cost, count):
        self.engine, self.name, self.emit, self.after, self.cost = engine, name, emit, after, cost
        self.count = count
        self.inc = 1 if count == engine else 16
        self.place = None
        self.plain = False


class Chain:

    def __init__(self, label):
        self.label, self.steps, self.by_name, self.total = label, [], {}, {}

    def step(self, engine, name, emit, after=(), cost=0.3, count=None, plain=False):
        assert name not in self.by_name, name
        s = Step(engine, name, emit, list(after), cost, count or engine)
        self.total[s.count] = self.total.get(s.count, 0) + 1
        s.place = self.total[s.count]
        s.plain = plain
        self.steps.append(s)
        self.by_name[name] = s
        return name

    def open(self, nc, ctx):
        self.sems = {k: ctx.enter_context(nc.semaphore(f"{self.label}_{k}_done")) for k in self.total}

    def value(self, name, start_ahead):
        before = isinstance(name, tuple)
        s = self.by_name[name[1] if before else name]
        n = self.total[s.count]
        at = s.place * s.inc + (n * s.inc if start_ahead else 0) - (n * s.inc if before else 0)
        return self.sems[s.count], n * s.inc, at, (s.count, before, s.place)


def run_queue(engine, queue, turns, known, start_ahead=True, unread=None):
    bases = {}
    for chain, s, shift in queue:
        need = {}
        for name in s.after:
            sem, per_sequence, value, (count, before, place) = chain.value(name, start_ahead)
            value += shift * per_sequence
            static = shift * chain.total[count] + place - (chain.total[count] if before else 0)
            if need.get(count, (None, None, None, -10**9))[3] < static:
                need[count] = (sem, per_sequence, value, static)
        for count, (sem, per_sequence, value, static) in need.items():
            if known.get((chain.label, count), -10**9) >= static:
                continue
            known[(chain.label, count)] = static
            turn = turns[chain.label]
            if not isinstance(turn, int):
                if (chain.label, count) not in bases:
                    bases[chain.label, count] = engine.snap(turn * per_sequence)
                engine.wait_ge(sem, bases[chain.label, count] + value)
            else:
                engine.wait_ge(sem, turn * per_sequence + value)
        if need and s.plain and start_ahead:
            engine.sem_inc(unread, 1)
        s.emit(engine, turns[chain.label] + shift).then_inc(chain.sems[s.count], s.inc)


def interleave(parts):
    engines = (PE, DVE, ACTE, POOL)
    lanes = {e: [[(c, s, sh) for c, s, sh in part if s.engine == e] for part in parts] for e in engines}
    free = dict.fromkeys(engines, 0.0)
    done = [dict() for _ in parts]
    pending = [set((s.name, sh) for _, s, sh in part) for part in parts]
    order = {e: [] for e in engines}
    while any(any(l) for ls in lanes.values() for l in [ls] if any(l)):
        best = None
        for e in engines:
            for k, lane in enumerate(lanes[e]):
                if not lane:
                    continue
                s, shift = lane[0][1:]
                deps = [(n, shift) for n in s.after if not isinstance(n, tuple)]
                deps = [n for n in deps if n in pending[k] or n in done[k]]
                if any(n not in done[k] for n in deps):
                    continue
                start = max([free[e]] + [done[k][n] + 0.1 for n in deps])
                if best is None or start < best[0]:
                    best = (start, e, k)
        start, e, k = best
        item = lanes[e][k].pop(0)
        free[e] = start + item[1].cost
        done[k][item[1].name, item[2]] = free[e]
        pending[k].discard((item[1].name, item[2]))
        order[e].append(item)
    return order


def spread(ap, dim, n):
    ap = ap.unsqueeze(dim)
    shape = list(ap.shape)
    shape[dim] = n
    return ap.broadcast_to(shape)


def windows(tile, w0, n):
    ap = tile[:, :, w0:w0 + T]
    return bass.AP(ap.tensor, ap.offset, [list(ap.ap[0]), [1, n], [T + 2 * PAD, KT], [1, T]])


def setup_steps(nc, st, sb, tmp, ps, inp, k):

    def load(name, dst, src):
        st.step(SP, name, lambda e, _: e.dma_start(dst, src), count=name)
        return name

    def dve(name, emit, *after):
        return st.step(DVE, name, lambda e, _: emit(e), after)

    def act(name, emit, *after):
        return st.step(ACTE, name, lambda e, _: emit(e), after)

    def pe(name, emit, *after):
        return st.step(PE, name, lambda e, _: emit(e), after)

    def tiles(ap):
        return ap.rearrange("(k p) n -> p k n", p=128)

    def rows(ap, p=128):
        return ap.partition_broadcast(p)

    for name, shape in (("wqkv0T", [128, KT, 3 * D]), ("wo0T", [128, KT, D]), ("wpT", [128, KT, D]),
                        ("w1aT", [128, KT, 128]), ("w1bT", [128, KT, 128]), ("wihT", [128, KT, GATES]),
                        ("wqkv1", [128, KT, 3 * D]), ("wproj", [128, KT, D]), ("wqkvxT", [128, KT, 3 * D]),
                        ("woxT", [128, KT, D])):
        k[name] = (tmp if name == "w1bT" else sb)(name, shape)
        load("ld_" + name, k[name][:], tiles(inp[name]))
    for name, shape in (("w2fT", [128, SLOTS]), ("ident", [128, 128]), ("parity", [128, 2]),
                        ("head_ones", [128, 8]), ("expand", [WIN * H, WIN * KT * 128])):
        k[name] = sb(name, shape)
        load("ld_" + name, k[name][:], inp[name])
    for name, src, n in (("bo0_r", "bo0", D), ("bp_r", "bp", D), ("bof_r", "bof", D), ("bproj_r", "bproj", D),
                         ("box_r", "box", D), ("bv1_r", "bv1", D), ("bvx_r", "bvx", D), ("b2f_r", "b2f", SLOTS)):
        k[name] = sb(name, [128, n])
        load("ld_" + name, k[name][:], rows(inp[src]))

    k["ident_bf"] = sb("ident_bf", [128, 128], BF16)
    dve("ident_bf", lambda e: e.tensor_copy(k["ident_bf"][:], k["ident"][:]), "ld_ident")
    k["ones"] = sb("ones", [128, 128])
    dve("ones", lambda e: e.memset(k["ones"][:], 1.0))
    k["ones_bf"] = sb("ones_bf", [128, 128], BF16)
    dve("ones_bf", lambda e: e.memset(k["ones_bf"][:], 1.0))
    k["neg_half"] = sb("neg_half", [128, 1])
    dve("neg_half", lambda e: e.memset(k["neg_half"][:], -0.5))

    for tag in ("1", "x"):
        q, b = tmp("bq_c" + tag, [128, KT]), tmp("bk_c" + tag, [128, KT])
        k["bq" + tag] = sb("bq" + tag, [128, KT])
        k["bk" + tag] = sb("bk" + tag, [128, KT, 2])
        load("ld_bq" + tag, q[:], inp["bq" + tag])
        load("ld_bk" + tag, b[:], inp["bk" + tag])
        dve("bq" + tag, lambda e, q=q, tag=tag: e.tensor_scalar(k["bq" + tag][:], q[:], -0.25, None, ALU.mult), "ld_bq" + tag)
        for o in range(2):
            dve(f"bk{tag}{o}", lambda e, b=b, tag=tag, o=o: e.tensor_scalar(
                k["bk" + tag][:, :, o], b[:], k["parity"][:, o:o + 1], None, ALU.mult), "ld_bk" + tag, "ld_parity")

    c = {}
    for name, shape in (("cw1", [H, 32]), ("cb1", [H, 32]), ("cw2", [H, 32, 32]), ("cb2", [H, 32]),
                        ("cw3", [H, 32]), ("cb3", [H, 1]), ("pos7", [H, WIN]), ("diag16", [H, WIN, H])):
        c[name] = tmp("c_" + name, shape)
        load("ld_" + name, c[name][:], inp[name])
    h1, h2, cw = tmp("conn_h1", [H, WIN, 32]), tmp("conn_h2", [H, WIN, 32]), tmp("conn_w", [H, WIN])
    z, cs, dg = tmp("conn_z", [H, WIN, 32, 32]), tmp("conn_s", [H, 1]), tmp("conn_d", [H, WIN, H])
    k["conn"] = sb("conn", [128, WIN * H])
    dve("conn1", lambda e: e.tensor_tensor(h1[:], spread(c["pos7"][:], 2, 32), spread(c["cw1"][:], 1, WIN), ALU.mult),
        "ld_pos7", "ld_cw1")
    dve("conn2", lambda e: e.tensor_tensor(h1[:], h1[:], spread(c["cb1"][:], 1, WIN), ALU.add), "conn1", "ld_cb1")
    act("conn3", lambda e: e.activation(h1[:], h1[:], ACT.Gelu), "conn2")
    dve("conn4", lambda e: e.tensor_tensor(z[:], spread(h1[:], 2, 32), spread(c["cw2"][:], 1, WIN), ALU.mult),
        "conn3", "ld_cw2")
    dve("conn5", lambda e: e.tensor_reduce(h2[:], z[:], AX.X, ALU.add), "conn4")
    dve("conn6", lambda e: e.tensor_tensor(h2[:], h2[:], spread(c["cb2"][:], 1, WIN), ALU.add), "conn5", "ld_cb2")
    act("conn7", lambda e: e.activation(h2[:], h2[:], ACT.Gelu), "conn6")
    dve("conn8", lambda e: e.tensor_tensor(h2[:], h2[:], spread(c["cw3"][:], 1, WIN), ALU.mult), "conn7", "ld_cw3")
    dve("conn9", lambda e: e.tensor_reduce(cw[:], h2[:], AX.X, ALU.add), "conn8")
    dve("conn10", lambda e: e.tensor_scalar(cw[:], cw[:], c["cb3"][:, 0:1], None, ALU.add), "conn9", "ld_cb3")
    dve("conn11", lambda e: e.tensor_reduce(cs[:], cw[:], AX.X, ALU.max, negate=True), "conn10")
    act("conn12", lambda e: e.activation(cw[:], cw[:], ACT.Exp, bias=cs[:, 0:1]), "conn11")
    dve("conn13", lambda e: e.tensor_reduce(cs[:], cw[:], AX.X, ALU.add), "conn12")
    dve("conn14", lambda e: e.reciprocal(cs[:], cs[:]), "conn13")
    dve("conn15", lambda e: e.tensor_scalar(cw[:], cw[:], cs[:, 0:1], None, ALU.mult), "conn14")
    dve("conn16", lambda e: e.tensor_tensor(dg[:], spread(cw[:], 2, H), c["diag16"][:], ALU.mult),
        "conn15", "ld_diag16")
    pe("conn17", lambda e: e.matmul(ps[:, 0, 0:WIN * H], k["ones"][0:H, :], dg[:].rearrange("p a b -> p (a b)"),
                                    start=True, stop=True), "conn16", "ones")
    dve("conn", lambda e: e.tensor_copy(k["conn"][:], ps[:, 0, 0:WIN * H]), "conn17")

    slot, scale = tmp("slot_init", [SLOTS, D]), tmp("slot_scale", [SLOTS, 1])
    load("ld_slot", slot[:], inp["slot_init"])
    load("ld_slot_scale", scale[:], inp["slot_scale"])
    whh, bhh, bih = tmp("whhT", [128, KT, GATES]), tmp("bhh_r", [SLOTS, GATES]), tmp("bih_r", [SLOTS, GATES])
    load("ld_whh", whh[:], tiles(inp["whhT"]))
    load("ld_bhh", bhh[:], rows(inp["bhh"], SLOTS))
    load("ld_bih", bih[:], rows(inp["bih"], SLOTS))
    b1c, meanT, slotT = tmp("b1_c", [128, 1]), tmp("slot_meanT", [128, KT]), tmp("slotT", [128, KT, SLOTS])
    load("ld_b1f", b1c[:], inp["b1f"])
    k["slots"] = sb("slots", [SLOTS, D])
    dve("slots", lambda e: e.tensor_scalar(k["slots"][:], slot[:], scale[:, 0:1], None, ALU.mult), "ld_slot", "ld_slot_scale")
    for j in range(KT):
        s_j = k["slots"][:, 128 * j:128 * j + 128]
        pe(f"slot_mean{j}", lambda e, s_j=s_j, j=j: e.matmul(ps[:, 1, j:j + 1], s_j, k["ones"][0:SLOTS, 0:1],
                                                             start=True, stop=True), "slots", "ones")
        pe(f"slotT{j}", lambda e, s_j=s_j, j=j: e.transpose(ps[:, 2, SLOTS * j:SLOTS * j + SLOTS], s_j,
                                                            k["ident"][0:SLOTS, 0:SLOTS]), "slots", "ld_ident")
    dve("slot_mean", lambda e: e.tensor_scalar(meanT[:], ps[:, 1, 0:KT], 1.0 / SLOTS, None, ALU.mult), "slot_mean1")
    dve("slotT", lambda e: e.tensor_copy(slotT[:], ps[:, 2, 0:KT * SLOTS].rearrange("p (k s) -> p k s", k=KT)), "slotT1")
    k["hid_bias"] = sb("hid_bias", [128, 1])
    for j in range(KT):
        pe(f"hid_bias{j}", lambda e, j=j: e.matmul(ps[:, 3, 0:1], k["w1bT"][:, j, :], meanT[:, j:j + 1],
                                                   start=(j == 0), stop=(j == KT - 1)), "slot_mean", "ld_w1bT")
    dve("hid_bias", lambda e: e.tensor_tensor(k["hid_bias"][:], ps[:, 3, 0:1], b1c[:], ALU.add), "hid_bias1", "ld_b1f")
    for a, n in ((0, 512), (512, 256)):
        for j in range(KT):
            pe(f"gh{a}_{j}", lambda e, a=a, n=n, j=j: e.matmul(
                ps[0:SLOTS, 4 + a // 512, 0:n], slotT[:, j, :], whh[:, j, a:a + n],
                start=(j == 0), stop=(j == KT - 1)), "slotT", "ld_whh")
    k["gate_bias"], k["half_hn"], k["new_bias"] = (sb("gate_bias", [SLOTS, 512]), sb("half_hn", [SLOTS, D]),
                                                   sb("new_bias", [SLOTS, D]))
    dve("gate_b1", lambda e: e.tensor_tensor(k["gate_bias"][:], ps[0:SLOTS, 4, :], bhh[:, 0:512], ALU.add),
        "gh0_1", "ld_bhh")
    dve("gate_b2", lambda e: e.tensor_tensor(k["gate_bias"][:], k["gate_bias"][:], bih[:, 0:512], ALU.add),
        "gate_b1", "ld_bih")
    dve("half_hn1", lambda e: e.tensor_tensor(k["half_hn"][:], ps[0:SLOTS, 5, 0:D], bhh[:, 512:768], ALU.add), "gh512_1")
    dve("half_hn2", lambda e: e.tensor_scalar(k["half_hn"][:], k["half_hn"][:], 0.5, None, ALU.mult), "half_hn1")
    dve("new_bias", lambda e: e.tensor_copy(k["new_bias"][:], bih[:, 512:768]), "ld_bih")

    wv, wo, bv, bvw = tmp("wvf", [128, KT, D]), tmp("wofT", [128, KT, D]), tmp("bvf_c", [128, KT]), tmp("bvf_w", [128, KT, SLOTS])
    load("ld_wvf", wv[:], tiles(inp["wvf"]))
    load("ld_wofT", wo[:], tiles(inp["wofT"]))
    load("ld_bvf", bv[:], inp["bvf"])
    k["wvo"], k["bvo"] = sb("wvo", [128, KT, D]), sb("bvo", [SLOTS, D])
    for i in range(KT):
        for j in range(KT):
            pe(f"wvo{i}{j}", lambda e, i=i, j=j: e.matmul(ps[:, 6, D * i:D * i + D], wv[:, j, 128 * i:128 * i + 128],
                                                          wo[:, j, :], start=(j == 0), stop=(j == KT - 1)),
               "ld_wvf", "ld_wofT")
    dve("wvo", lambda e: e.tensor_copy(k["wvo"][:], ps[:, 6, :].rearrange("p (k n) -> p k n", k=KT)), "wvo11")
    for j in range(KT):
        dve(f"bvw{j}", lambda e, j=j: e.tensor_scalar(bvw[:, j, :], k["ones"][:, 0:SLOTS], bv[:, j:j + 1], None, ALU.mult),
            "ones", "ld_bvf")
    for j in range(KT):
        pe(f"bvo{j}", lambda e, j=j: e.matmul(ps[0:SLOTS, 7, 0:D], bvw[:, j, :], wo[:, j, :],
                                              start=(j == 0), stop=(j == KT - 1)), "bvw1")
    dve("bvo", lambda e: e.tensor_copy(k["bvo"][:], ps[0:SLOTS, 7, 0:D]), "bvo1")
    tau = tmp("tau_c", [128, 1])
    k["inv_tau"] = sb("inv_tau", [128, 1])
    load("ld_tau", tau[:], rows(inp["tau"]))
    act("tau1", lambda e: e.activation(tau[:], tau[:], ACT.Abs), "ld_tau")
    dve("tau2", lambda e: e.tensor_scalar(tau[:], tau[:], 0.1, None, ALU.add), "tau1")
    dve("inv_tau", lambda e: e.reciprocal(k["inv_tau"][:], tau[:]), "tau2")

    rel, pos, w1c, b1w = tmp("rel", [128, 32, T]), tmp("pos", [128, T]), tmp("fw1", [128, 1]), tmp("fb1", [128, 1])
    w2c, b2r, cau = tmp("fw2", [128, H]), tmp("fb2_r", [128, H]), tmp("causal", [128, T])
    cpar, lmul = tmp("cpar", [128, 1]), tmp("lmul", [128, 1])
    load("ld_rel", rel[:].rearrange("p a b -> p (a b)"), inp["rel"])
    load("ld_pos", pos[:], inp["pos"])
    load("ld_causal", cau[:], inp["causal"])
    load("ld_cpar", cpar[:], rows(inp["c_param"]))
    load("ld_lmul", lmul[:], rows(inp["l_mult"]))
    load("ld_fb2", b2r[:], rows(inp["fb2"]))
    for g in range(4):
        load(f"ld_fw1{g}", w1c[32 * g:32 * g + 32, :], inp["fw1"])
        load(f"ld_fb1{g}", b1w[32 * g:32 * g + 32, :], inp["fb1"])
        load(f"ld_fw2{g}", w2c[32 * g:32 * g + 32, :], inp["fw2"])
    act("fire1", lambda e: e.activation(rel[:], rel[:], ACT.Abs, scale=cpar[:, 0:1]), "ld_rel", "ld_cpar")
    act("fire2", lambda e: e.activation(lmul[:], lmul[:], ACT.Abs, scale=512.0), "ld_lmul")
    dve("fire3", lambda e: e.tensor_scalar(pos[:], pos[:], lmul[:, 0:1], None, ALU.max), "fire2", "ld_pos")
    act("fire4", lambda e: e.activation(pos[:], pos[:], ACT.Abs, scale=cpar[:, 0:1]), "fire3")
    act("fire5", lambda e: e.activation(pos[:], pos[:], ACT.Ln, bias=1.0), "fire4")
    act("fire6", lambda e: e.activation(rel[:], rel[:], ACT.Ln, bias=1.0), "fire1")
    dve("fire7", lambda e: e.tensor_scalar(pos[:], pos[:], 1e-6, None, ALU.add), "fire5")
    dve("fire8", lambda e: e.reciprocal(pos[:], pos[:]), "fire7")
    dve("fire9", lambda e: e.tensor_tensor(rel[:], rel[:], spread(pos[:], 1, 32), ALU.mult), "fire6", "fire8")
    act("fire10", lambda e: e.activation(rel[:], rel[:], ACT.Relu, scale=w1c[:, 0:1], bias=b1w[:, 0:1]),
        "fire9", *[f"ld_fw1{g}" for g in range(4)], *[f"ld_fb1{g}" for g in range(4)])
    dve("fire11", lambda e: e.tensor_scalar(w2c[:], w2c[:], -1.0, None, ALU.mult), *[f"ld_fw2{g}" for g in range(4)])
    dve("fire12", lambda e: e.tensor_scalar(b2r[:], b2r[:], -1.0, None, ALU.mult), "ld_fb2")
    k["pos_bias"] = sb("pos_bias", [128, GROUPS, KT, 2, T])
    fb = tmp("fire_b", [128, 4, 32, H])
    for g in range(4):
        for s in range(32):
            pe(f"fire_mm{g}_{s}", lambda e, g=g, s=s: e.matmul(
                ps[:, g, H * s:H * s + H], rel[32 * g:32 * g + 32, s, :], w2c[32 * g:32 * g + 32, :],
                start=True, stop=True), "fire10", "fire11", "conn", "slot_mean", "slotT", "hid_bias",
                *([f"fire_b{g - 1}"] if g else []))
        dve(f"fire_b{g}", lambda e, g=g: e.tensor_tensor(
            fb[:, g, :, :], ps[:, g, :].rearrange("p (s h) -> p s h", h=H), spread(b2r[:], 1, 32), ALU.add),
            f"fire_mm{g}_31", "fire12")
        for j in range(KT):
            for q in range(GROUPS):
                dve(f"pos_bias{g}{j}{q}", lambda e, g=g, j=j, q=q: e.tensor_tensor(
                    k["pos_bias"][:, q, j, :, 32 * g:32 * g + 32],
                    fb[:, g, :, 8 * j + 2 * q:8 * j + 2 * q + 2].rearrange("p s o -> p o s"),
                    spread(cau[:, 32 * g:32 * g + 32], 1, 2), ALU.add), f"fire_b{g}", "ld_causal")

    for name, n, shape in (("w1t", HID * KT, [128, KT, HID]), ("w2t", HT * D, [128, HT, D])):
        w, a = tmp("f_" + name, [128, n]), tmp("a_" + name, [128, 1])
        k[name] = sb(name, [128, n], BF16)
        k[name + "_mean"] = sb(name + "_mean", [128, 1])
        bank = 6 if name == "w1t" else 7
        load("ld_" + name, w[:].rearrange("p (k n) -> p k n", k=shape[1]), tiles(inp[name]))
        dve(name + "1", lambda e, w=w, a=a: e.tensor_reduce(a[:], w[:], AX.X, ALU.add, apply_absolute_value=True), "ld_" + name)
        pe(name + "2", lambda e, a=a, bank=bank: e.matmul(ps[:, bank, 0:1], k["ones"][:], a[:], start=True, stop=True),
           name + "1", "wvo", "bvo")
        dve(name + "3", lambda e, name=name, bank=bank: e.tensor_scalar(
            k[name + "_mean"][:], ps[:, bank, 0:1], 1.0 / (HID * D), 1e-5, ALU.mult, ALU.max), name + "2")
        dve(name + "4", lambda e, name=name, a=a: e.reciprocal(a[:], k[name + "_mean"][:]), name + "3")
        dve(name + "5", lambda e, w=w, a=a: e.tensor_scalar(w[:], w[:], a[:, 0:1], ROUND, ALU.mult, ALU.add), name + "4")
        dve(name + "6", lambda e, w=w: e.tensor_scalar(w[:], w[:], -ROUND, 1.0, ALU.add, ALU.min), name + "5")
        dve(name + "7", lambda e, w=w, name=name: e.tensor_scalar(k[name][:], w[:], -1.0, None, ALU.max), name + "6")
    for name, f in (("w1t", 1.0 / 127), ("w2t", 0.5 / 127)):
        k[name + "_back"] = sb(name + "_back", [128, 1])
        dve(name + "_back", lambda e, name=name, f=f: e.tensor_scalar(
            k[name + "_back"][:], k[name + "_mean"][:], f, None, ALU.mult), name + "3")
    for name in ("conv_w", "conv_b"):
        k[name] = sb(name, [128, HT, 3] if name == "conv_w" else [128, HT])
        load("ld_" + name, k[name][:], inp[name])


def buffers(nc, sb, label):
    t = {}
    for name, shape, dt in (
        ("x_in", [128, D], F32), ("ctx", [128, D], F32), ("mask_r", [128, T], F32), ("mask_c", [128, 1], F32),
        ("mask_bf", [128, T], BF16), ("xb", [128, D], F32), ("xa", [128, D], F32), ("xn", [128, D], F32),
        ("xnT", [128, KT, T], F32), ("ctxT", [128, KT, T], F32), ("stat", [128, 8], F32), ("sv", [128, 4], F32),
        ("qT", [128, KT, T], F32), ("kp", [128, KT, T + 2 * PAD], F32), ("vp", [128, KT, T + 2 * PAD], F32),
        ("prod", [128, WIN, KT, T], F32), ("wsc", [128, WIN, H], F32), ("wsm", [128, 5, H], F32),
        ("fwT", [WIN * H, T], F32), ("kx", [128, KT, 2, T], F32), ("va", [128, H, VC], F32),
        ("neg_min", [128, GROUPS, PER], F32), ("sums", [128, H], F32), ("o", [128, D], F32),
        ("oT", [128, KT, T], F32), ("out", [128, D], F32),
        ("lg", [128, 3, SLOTS], F32), ("top", [128, 8], F32), ("sc1", [128, 4], F32), ("hT", [128, T], F32),
        ("al", [128, SLOTS], F32), ("alT", [SLOTS, T], F32), ("giT", [128, KT, SLOTS], F32), ("rws", [SLOTS, 2], F32),
        ("rz", [SLOTS, 512], F32), ("nw", [SLOTS, 3, D], F32), ("hnT", [128, KT, SLOTS], F32), ("sval", [SLOTS, D], F32),
        ("xq", [128, D], F32), ("xqb", [128, D], BF16), ("xqT", [128, KT, T], BF16), ("qs", [128, 8], F32),
        ("dg", [128, T], F32), ("back", [128, T], F32), ("hp", [128, HT, T + 2], F32), ("cv", [128, HT, T], F32),
        ("hid", [128, HT, T], F32), ("hqb", [128, HID], BF16), ("hqT", [128, HT, T], BF16),
    ):
        t[name] = sb(f"{label}_{name}", shape, dt)
    t["s"] = sb(f"{label}_s", [128, 2, PER * T], F32)
    t["p"] = sb(f"{label}_p", [128, 2, PER, T], F32)
    t["pT"] = sb(f"{label}_pT", [128, 2, PER, T], F32)
    return t


def sequence_steps(ch, t, ps, k, dram):

    def dve(name, emit, *after, n=256, plain=False):
        return ch.step(DVE, name, lambda e, _: emit(e), after, cost=0.07 + n / 960, plain=plain)

    def act(name, emit, *after, n=256):
        return ch.step(ACTE, name, lambda e, _: emit(e), after, cost=0.1 + n / 1200)

    def pool(name, emit, *after, n=256, plain=False):
        return ch.step(POOL, name, lambda e, _: emit(e), after, cost=0.1 + n / 450, plain=plain)

    def mm(name, out, lhsT, rhs, *after, start=True, stop=True, passes=4, skip=False):
        n = max(64, rhs.free_size())
        return ch.step(PE, name, lambda e, _: e.matmul(out, lhsT, rhs, start=start, stop=stop, skip_group_check=skip),
                       after, cost=passes * n / 2400)

    def flip(name, out, src, *after, ident=None):
        rows = src.shape[0]
        ident = (k["ident"] if ident is None else ident)[0:rows, 0:rows]
        return ch.step(PE, name, lambda e, _: e.transpose(out, src, ident), after, cost=0.11, plain=rows < 128)

    def layer_norm(tag, x, ready, bank_free):
        dve(tag + "_st", lambda e: e.bn_stats(t["stat"][:, 0:6], x), *ready)
        dve(tag + "_mv", lambda e: e.bn_aggr(t["sv"][:, 0:2], t["stat"][:, 0:6]), tag + "_st", n=8, plain=True)
        dve(tag + "_ve", lambda e: e.tensor_scalar(t["sv"][:, 2:3], t["sv"][:, 1:2], LN_EPS, None, ALU.add), tag + "_mv", n=8)
        ch.step(POOL, tag + "_rs", lambda e, _: e.tensor_tensor(t["sv"][:, 3:4], t["sv"][:, 2:3], k["neg_half"][:], ALU.pow),
                [tag + "_ve"], cost=1.0)
        dve(tag + "_xn", lambda e: e.tensor_scalar(t["xn"][:], x, t["sv"][:, 0:1], t["sv"][:, 3:4],
                                                   ALU.subtract, ALU.mult), tag + "_rs")
        for j in range(KT):
            flip(f"{tag}_T{j}", ps[:, 3, T * j:T * j + T], t["xn"][:, 128 * j:128 * j + 128], tag + "_xn", *bank_free)

    def copy_xnT(tag):
        act(tag + "_xnT", lambda e: e.copy(t["xnT"][:], ps[:, 3, 0:D].rearrange("p (k t) -> p k t", k=KT)), f"{tag}_T1")

    def residual_in(tag, x, bias, ready):
        pool(tag + "_xb", lambda e: e.tensor_tensor(t["xb"][:], x, bias[:], ALU.add), *ready)

    def project(tag, w, lhsT, bank, ready):
        for j in range(KT):
            mm(f"{tag}_pr{j}", ps[:, bank, 0:D], lhsT[:, j, :], w[:, j, :], *ready, start=(j == 0), stop=(j == KT - 1))

    def attention(tag, ready, bias=None, masked=False, scale_rows=False):

        def scores(g):
            bank, r = g % 2, 32 * g
            free = [f"{tag}_ex{g - 2}_{PER - 1}" if bias is None else f"{tag}_bi{g - 2}"] if g >= 2 else []
            for j in range(KT):
                out = ps[:, bank, D * j:D * j + D]
                if masked:
                    mm(f"{tag}_mk{g}{j}", out, k["ones_bf"][r:r + 1, :], spread(t["mask_bf"][r:r + 1, :], 1, 2),
                       "mask_bf", *ready, *free, stop=False, passes=1)
                mm(f"{tag}_s{g}{j}", out, t["qT"][r:r + 32, j, :], t["kx"][r:r + 32, j, :, :].rearrange("p o t -> p (o t)"),
                   *ready, *free, start=not masked)
            src = ps[:, bank, :]
            last = f"{tag}_s{g}1"
            if bias is not None:
                dve(f"{tag}_bi{g}", lambda e: e.tensor_tensor(
                    t["s"][:, bank, :], ps[:, bank, :], bias[:, g, :, :, :].rearrange("p j o t -> p (j o t)"), ALU.add),
                    last, *([f"{tag}_ex{g - 2}_{PER - 1}"] if g >= 2 else []), n=512)
                src, last = t["s"][:, bank, :], f"{tag}_bi{g}"
            src = src.rearrange("p (a t) -> p a t", t=T)
            dve(f"{tag}_mx{g}", lambda e: e.tensor_reduce(t["neg_min"][:, g, :], src, AX.X, ALU.min), last, n=512)
            for a in range(PER):
                act(f"{tag}_ex{g}_{a}", lambda e, a=a: e.activation(
                    t["p"][:, g % 2, a, :], src[:, a, :], ACT.Exp, scale=-1.0, bias=t["neg_min"][:, g, a:a + 1]),
                    f"{tag}_mx{g}", *([f"{tag}_pT{g - 2}_{PER - 1}"] if g >= 2 else []), n=200)

        def turn(g):
            for a in range(PER):
                flip(f"{tag}_pT{g}_{a}", ps[:, 2, T * a:T * a + T], t["p"][:, g % 2, a, :], f"{tag}_ex{g}_{a}",
                     *([f"{tag}_pc{g - 1}"] if g else []))
            dve(f"{tag}_pc{g}", lambda e: e.tensor_copy(t["pT"][:, g % 2, :, :].rearrange("p a t -> p (a t)"), ps[:, 2, :]),
                f"{tag}_pT{g}_{PER - 1}", *([f"{tag}_pv{g - 2}_{PER - 1}"] if g >= 2 else []), n=512)

        def values(g):
            for a in range(PER):
                h = 8 * (a // 2) + 2 * g + a % 2
                mm(f"{tag}_pv{g}_{a}", ps[:, 3, VC * h:VC * h + VC], t["pT"][:, g % 2, a, :], t["va"][:, h, :],
                   f"{tag}_pc{g}", *ready)

        scores(0)
        scores(1)
        for g in range(GROUPS):
            turn(g)
            if g + 2 < GROUPS:
                scores(g + 2)
            values(g)
        o = ps[:, 3, 0:H * VC].rearrange("p (h c) -> p h c", c=VC)
        dve(tag + "_rc", lambda e: e.reciprocal(t["sums"][:], o[:, :, DH]), f"{tag}_pv{GROUPS - 1}_{PER - 1}", n=16)
        norm = tag + "_rc"
        if scale_rows:
            dve(tag + "_rm", lambda e: e.tensor_scalar(t["sums"][:], t["sums"][:], t["mask_c"][:, 0:1], None, ALU.mult),
                norm, "mask_c", n=16)
            norm = tag + "_rm"
        dve(tag + "_o", lambda e: e.tensor_tensor(t["o"][:].rearrange("p (h c) -> p h c", c=DH), o[:, :, 0:DH],
                                                  spread(t["sums"][:], 2, DH), ALU.mult), norm)
        for j in range(KT):
            flip(f"{tag}_oT{j}", ps[:, 0, T * j:T * j + T], t["o"][:, 128 * j:128 * j + 128], tag + "_o")
        act(tag + "_oc", lambda e: e.copy(t["oT"][:], ps[:, 0, 0:D].rearrange("p (k t) -> p k t", k=KT)), f"{tag}_oT1")

    def keys(tag, src, ready, bias=None):
        for o in range(2):
            if bias is None:
                act(f"{tag}_kx{o}", lambda e, o=o: e.activation(t["kx"][:, :, o, :], src, ACT.Copy,
                                                               scale=k["parity"][:, o:o + 1]), *ready)
                continue
            for j in range(KT):
                act(f"{tag}_kx{o}{j}", lambda e, o=o, j=j: e.activation(
                    t["kx"][:, j, o, :], src[:, j, :], ACT.Identity, scale=k["parity"][:, o:o + 1],
                    bias=bias[:, j, o:o + 1]), *ready, n=250)

    first = ("before", "y")

    layer_norm("a", t["x_in"][:], ["x_in", first], [first])
    copy_xnT("a")
    residual_in("a", t["x_in"][:], k["bo0_r"], ["x_in", first])
    for i, part in enumerate("qkv"):
        for m in range(KT):
            for j in range(KT):
                c0 = D * i + 128 * m
                out = ps[:, 0 if i < 2 else 1, D * (i % 2) + T * m:D * (i % 2) + T * m + T]
                mm(f"a_{part}{m}{j}", out, k["wqkv0T"][:, j, c0:c0 + 128], t["xnT"][:, j, :], "a_xnT",
                   start=(j == 0), stop=(j == KT - 1))
    act("a_qT", lambda e: e.copy(t["qT"][:], ps[:, 0, 0:D].rearrange("p (k t) -> p k t", k=KT)), "a_k11")
    act("a_kp", lambda e: e.copy(t["kp"][:, :, PAD:PAD + T], ps[:, 0, D:2 * D].rearrange("p (k t) -> p k t", k=KT)), "a_k11")
    act("a_vp", lambda e: e.copy(t["vp"][:, :, PAD:PAD + T], ps[:, 1, 0:D].rearrange("p (k t) -> p k t", k=KT)), "a_v11")
    WD = 5
    dve("a_qk", lambda e: e.tensor_tensor(t["prod"][:, 0:WD], spread(t["qT"][:], 1, WD), windows(t["kp"], 0, WD), ALU.mult),
        "a_qT", "a_kp", n=256 * WD)
    pool("a_qk2", lambda e: e.tensor_tensor(t["prod"][:, WD:WIN], spread(t["qT"][:], 1, WIN - WD),
                                            windows(t["kp"], WD, WIN - WD), ALU.mult), "a_qT", "a_kp", n=256 * (WIN - WD))
    for w in range(WIN):
        for j in range(KT):
            mm(f"a_sc{w}{j}", ps[:, 2, H * w + 8 * j:H * w + 8 * j + 8], t["prod"][:, w, j, :], k["head_ones"][:],
               "a_qk" if w < WD else "a_qk2")
    sc = ps[:, 2, 0:WIN * H].rearrange("p (w h) -> p w h", h=H)
    sm, ws = t["wsm"], t["wsc"]
    by_head = ws[:].rearrange("p w h -> p h w")
    dve("a_mx", lambda e: e.tensor_reduce(sm[:, 0, :], sc.rearrange("p w h -> p h w"), AX.X, ALU.max), "a_sc61", n=112)
    dve("a_sub", lambda e: e.tensor_tensor(ws[:], sc, spread(sm[:, 0, :], 1, WIN), ALU.subtract), "a_mx", n=112)
    act("a_exp", lambda e: e.activation(ws[:], ws[:], ACT.Exp, scale=0.25), "a_sub", n=112)
    dve("a_sum", lambda e: e.tensor_reduce(sm[:, 1, :], by_head, AX.X, ALU.add), "a_exp", n=112)
    dve("a_cn", lambda e: e.tensor_tensor(ws[:], ws[:], k["conn"][:].rearrange("p (w h) -> p w h", h=H), ALU.mult),
        "a_exp", "a_sum", n=112)
    dve("a_sumc", lambda e: e.tensor_reduce(sm[:, 2, :], by_head, AX.X, ALU.add), "a_cn", n=112)
    dve("a_den", lambda e: e.scalar_tensor_tensor(out=sm[:, 3, :], in0=sm[:, 1, :], scalar=1e-9, in1=sm[:, 2, :],
                                                  op0=ALU.mult, op1=ALU.add), "a_sumc", n=16)
    dve("a_rec", lambda e: e.reciprocal(sm[:, 4, :], sm[:, 3, :]), "a_den", n=16)
    dve("a_fw", lambda e: e.tensor_tensor(ws[:], ws[:], spread(sm[:, 4, :], 1, WIN), ALU.mult), "a_rec", n=112)
    flip("a_fT", ps[0:WIN * H, 3, 0:T], ws[:].rearrange("p w h -> p (w h)"), "a_fw", "a_xnT")
    act("a_fc", lambda e: e.copy(t["fwT"][:], ps[0:WIN * H, 3, 0:T]), "a_fT", n=128)
    for q in range(4):
        n = min(2, WIN - 2 * q)
        for w in range(2 * q, 2 * q + n):
            for j in range(KT):
                c0 = D * (w % 2) + T * j
                mm(f"a_e{w}{j}", ps[:, q, c0:c0 + T], k["expand"][:, (w * KT + j) * 128:(w * KT + j) * 128 + 128],
                   t["fwT"][:], "a_fc", "a_vp", "a_sub")
        dve(f"a_pv{q}", lambda e, q=q, n=n: e.tensor_tensor(
            t["prod"][:, 2 * q:2 * q + n], ps[:, q, 0:D * n].rearrange("p (w j t) -> p w j t", w=n, j=KT),
            windows(t["vp"], 2 * q, n), ALU.mult), f"a_e{2 * q + n - 1}1", n=256 * n)
    dve("a_o3", lambda e: e.tensor_tensor(t["prod"][:, 0:3], t["prod"][:, 0:3], t["prod"][:, 3:6], ALU.add), "a_pv2", n=768)
    pool("a_o1", lambda e: e.tensor_tensor(t["prod"][:, 6], t["prod"][:, 6], t["prod"][:, 0], ALU.add), "a_pv3", "a_o3")
    dve("a_o2", lambda e: e.tensor_tensor(t["prod"][:, 1], t["prod"][:, 1], t["prod"][:, 2], ALU.add), "a_o3")
    dve("a_oT", lambda e: e.tensor_tensor(t["oT"][:], t["prod"][:, 1], t["prod"][:, 6], ALU.add), "a_o2", "a_o1")
    project("a", k["wo0T"], t["oT"], 0, ["a_oT"])
    dve("a_y", lambda e: e.tensor_tensor(t["xa"][:], ps[:, 0, 0:D], t["xb"][:], ALU.add), "a_pr1", "a_xb")

    layer_norm("b", t["xa"][:], ["a_y"], ["a_pv3"])
    act("b_q", lambda e: e.activation(t["qT"][:], ps[:, 3, 0:D].rearrange("p (k t) -> p k t", k=KT), ACT.Copy, scale=-0.25),
        "b_T1")
    for j in range(KT):
        flip(f"c_T{j}", ps[:, 2, T * j:T * j + T], t["ctx"][:, 128 * j:128 * j + 128], "ctx", "a_pv2")
    act("c_T", lambda e: e.copy(t["ctxT"][:], ps[:, 2, 0:D].rearrange("p (k t) -> p k t", k=KT)), "c_T1")
    keys("b", t["ctxT"][:], ["c_T"])
    dve("mask_bf", lambda e: e.tensor_scalar(t["mask_bf"][:], t["mask_r"][:], 0.0, MASKED, ALU.is_equal, ALU.mult),
        "mask_r", first, n=128)
    va_cols = t["va"][:, :, 0:DH]
    dve("b_va", lambda e: e.tensor_scalar(va_cols, t["ctx"][:].rearrange("p (h c) -> p h c", c=DH), t["mask_c"][:, 0:1], None,
                                          ALU.mult), "ctx", "mask_c", first)
    pool("b_xb1", lambda e: e.tensor_scalar(t["out"][:], k["bp_r"][:], t["mask_c"][:, 0:1], 0.0, ALU.mult, ALU.add),
         "mask_c", ("before", "store"), plain=True)
    pool("b_xb", lambda e: e.tensor_tensor(t["xb"][:], t["xa"][:], t["out"][:], ALU.add), "b_xb1", "a_y")
    attention("b", ["b_q", "b_kx1", "b_va"], masked=True, scale_rows=True)
    project("b", k["wpT"], t["oT"], 1, ["b_oc"])
    dve("b_y", lambda e: e.scalar_tensor_tensor(out=t["xa"][:], in0=ps[:, 1, 0:D], scalar=t["mask_c"][:, 0:1],
                                                in1=t["xb"][:], op0=ALU.mult, op1=ALU.add), "b_pr1", "b_xb")

    layer_norm("f", t["xa"][:], ["b_y"], ["b_o"])
    copy_xnT("f")
    residual_in("f", t["xa"][:], k["bof_r"], ["b_y"])
    for j in range(KT):
        mm(f"f_h{j}", ps[:, 0, 0:T], k["w1aT"][:, j, :], t["xnT"][:, j, :], "f_xnT", start=(j == 0), stop=(j == KT - 1))
    act("f_gelu", lambda e: e.activation(t["hT"][:], ps[:, 0, 0:T], ACT.Gelu, bias=k["hid_bias"][:, 0:1]), "f_h1", n=1500)
    mm("f_lg", ps[:, 1, 0:SLOTS], t["hT"][:], k["w2fT"][:], "f_gelu")
    lg = t["lg"]
    dve("f_l", lambda e: e.tensor_tensor(lg[:, 0, :], ps[:, 1, 0:SLOTS], k["b2f_r"][:], ALU.add), "f_lg", n=64)
    dve("f_top", lambda e: e.max(t["top"][:], lg[:, 0, :]), "f_l", n=64, plain=True)
    dve("f_mr", lambda e: e.match_replace(lg[:, 1, :], t["top"][:], lg[:, 0, :], -3e38), "f_top", n=128, plain=True)
    dve("f_nm", lambda e: e.tensor_scalar(t["sc1"][:, 0:1], t["top"][:, 0:1], k["inv_tau"][:, 0:1], -1.0, ALU.mult, ALU.mult),
        "f_top", n=8)
    act("f_e", lambda e: e.activation(lg[:, 2, :], lg[:, 0, :], ACT.Exp, scale=k["inv_tau"][:, 0:1], bias=t["sc1"][:, 0:1]),
        "f_nm", n=200)
    dve("f_m", lambda e: e.tensor_tensor(lg[:, 1, :], lg[:, 1, :], lg[:, 0, :], ALU.is_lt), "f_mr", n=64)
    dve("f_em", lambda e: e.tensor_tensor(lg[:, 2, :], lg[:, 2, :], lg[:, 1, :], ALU.mult), "f_m", "f_e", n=64)
    dve("f_s", lambda e: e.tensor_reduce(t["sc1"][:, 1:2], lg[:, 2, :], AX.X, ALU.add), "f_em", n=64)
    dve("f_r", lambda e: e.reciprocal(t["sc1"][:, 2:3], t["sc1"][:, 1:2]), "f_s", n=8)
    dve("f_al", lambda e: e.tensor_scalar(t["al"][:], lg[:, 2, :], t["sc1"][:, 2:3], None, ALU.mult), "f_r", n=64)
    for j in range(KT):
        mm(f"f_gi{j}", ps[:, 2, SLOTS * j:SLOTS * j + SLOTS], t["xn"][:, 128 * j:128 * j + 128], t["al"][:], "f_al")
    mm("f_ws", ps[0:SLOTS, 1, 64:65], t["al"][:], k["ones"][:, 0:1], "f_al")
    flip("f_alT", ps[0:SLOTS, 0, 0:T], t["al"][:], "f_al")
    act("f_giT", lambda e: e.copy(t["giT"][:], ps[:, 2, 0:KT * SLOTS].rearrange("p (k s) -> p k s", k=KT)), "f_gi1", n=128)
    dve("f_w1", lambda e: e.tensor_scalar(t["rws"][:, 0:1], ps[0:SLOTS, 1, 64:65], 1e-8, None, ALU.add), "f_ws", n=8)
    dve("f_w2", lambda e: e.reciprocal(t["rws"][:, 1:2], t["rws"][:, 0:1]), "f_w1", n=8)
    act("f_ac", lambda e: e.copy(t["alT"][:], ps[0:SLOTS, 0, 0:T]), "f_alT", n=128)
    for a, n, bank in ((0, 512, 2), (512, 256, 3)):
        for j in range(KT):
            mm(f"f_gx{a}_{j}", ps[0:SLOTS, bank, 0:n], t["giT"][:, j, :], k["wihT"][:, j, a:a + n], "f_giT",
               start=(j == 0), stop=(j == KT - 1))
    dve("f_rz1", lambda e: e.scalar_tensor_tensor(out=t["rz"][:], in0=ps[0:SLOTS, 2, :], scalar=t["rws"][:, 1:2],
                                                  in1=k["gate_bias"][:], op0=ALU.mult, op1=ALU.add), "f_gx0_1", "f_w2", n=512)
    act("f_rz", lambda e: e.activation(t["rz"][:], t["rz"][:], ACT.Tanh, scale=0.5), "f_rz1", n=512)
    nw, tr, tz = t["nw"], t["rz"][:, 0:D], t["rz"][:, D:2 * D]
    dve("f_n1", lambda e: e.scalar_tensor_tensor(out=nw[:, 0, :], in0=ps[0:SLOTS, 3, 0:D], scalar=t["rws"][:, 1:2],
                                                 in1=k["new_bias"][:], op0=ALU.mult, op1=ALU.add), "f_gx512_1")
    dve("f_n2", lambda e: e.scalar_tensor_tensor(out=nw[:, 1, :], in0=tr, scalar=1.0, in1=k["half_hn"][:],
                                                 op0=ALU.add, op1=ALU.mult), "f_rz")
    dve("f_n3", lambda e: e.tensor_tensor(nw[:, 1, :], nw[:, 1, :], nw[:, 0, :], ALU.add), "f_n2", "f_n1")
    act("f_n", lambda e: e.activation(nw[:, 0, :], nw[:, 1, :], ACT.Tanh), "f_n3")
    dve("f_u1", lambda e: e.tensor_tensor(nw[:, 1, :], k["slots"][:], nw[:, 0, :], ALU.subtract), "f_n")
    dve("f_u2", lambda e: e.scalar_tensor_tensor(out=nw[:, 2, :], in0=tz, scalar=1.0, in1=nw[:, 1, :],
                                                 op0=ALU.add, op1=ALU.mult), "f_u1")
    dve("f_u3", lambda e: e.scalar_tensor_tensor(out=nw[:, 1, :], in0=nw[:, 2, :], scalar=0.5, in1=nw[:, 0, :],
                                                 op0=ALU.mult, op1=ALU.add), "f_u2")
    for j in range(KT):
        flip(f"f_hT{j}", ps[:, 0, SLOTS * j:SLOTS * j + SLOTS], nw[:, 1, 128 * j:128 * j + 128], "f_u3", "f_ac")
    act("f_hc", lambda e: e.copy(t["hnT"][:], ps[:, 0, 0:KT * SLOTS].rearrange("p (k s) -> p k s", k=KT)), "f_hT1", n=128)
    for j in range(KT):
        mm(f"f_sv{j}", ps[0:SLOTS, 1, 0:D], t["hnT"][:, j, :], k["wvo"][:, j, :], "f_hc", "f_w1",
           start=(j == 0), stop=(j == KT - 1))
    dve("f_sv", lambda e: e.tensor_tensor(t["sval"][:], ps[0:SLOTS, 1, 0:D], k["bvo"][:], ALU.add), "f_sv1")
    mm("f_o", ps[:, 0, 0:D], t["alT"][:], t["sval"][:], "f_sv", "f_ac", "f_hc")
    dve("f_y", lambda e: e.tensor_tensor(t["xa"][:], ps[:, 0, 0:D], t["xb"][:], ALU.add), "f_o", "f_xb")

    def dense_qkv(tag, w, kv, ready, bias_v):
        for i, src, bank in ((0, t["xnT"], 0), (1, kv, 1)):
            for m in range(KT):
                for j in range(KT):
                    mm(f"{tag}_{'qk'[i]}{m}{j}", ps[:, bank, T * m:T * m + T], w[:, j, D * i + 128 * m:D * i + 128 * m + 128],
                       src[:, j, :], *ready, start=(j == 0), stop=(j == KT - 1))
        for j in range(KT):
            mm(f"{tag}_v{j}", ps[:, 2, 0:D], kv[:, j, :], w[:, j, 2 * D:3 * D], *ready, start=(j == 0), stop=(j == KT - 1))
        for m in range(KT):
            act(f"{tag}_qc{m}", lambda e, m=m: e.activation(
                t["qT"][:, m, :], ps[:, 0, T * m:T * m + T], ACT.Identity, scale=-0.25, bias=k["bq" + tag][:, m:m + 1]),
                f"{tag}_q11", n=200)
        keys(tag, ps[:, 1, 0:D].rearrange("p (k t) -> p k t", k=KT), [f"{tag}_k11"], bias=k["bk" + tag])
        dve(tag + "_va", lambda e: e.tensor_tensor(va_cols, ps[:, 2, 0:D].rearrange("p (h c) -> p h c", c=DH),
                                                   bias_v[:].rearrange("p (h c) -> p h c", c=DH), ALU.add), f"{tag}_v1")

    layer_norm("n", t["xa"][:], ["f_y"], ["f_n1"])
    copy_xnT("n")
    residual_in("n", t["xa"][:], k["bproj_r"], ["f_y"])
    dense_qkv("1", k["wqkv1"], t["xnT"], ["n_xnT"], k["bv1_r"])
    attention("1", ["1_qc1", "1_kx11", "1_va"], bias=k["pos_bias"])
    project("1", k["wproj"], t["oT"], 1, ["1_oc"])
    dve("1_y", lambda e: e.tensor_tensor(t["xa"][:], ps[:, 1, 0:D], t["xb"][:], ALU.add), "1_pr1", "n_xb")

    layer_norm("m", t["xa"][:], ["1_y"], ["1_o"])
    copy_xnT("m")
    residual_in("m", t["xa"][:], k["box_r"], ["1_y"])
    dense_qkv("x", k["wqkvxT"], t["ctxT"], ["m_xnT"], k["bvx_r"])
    attention("x", ["x_qc1", "x_kx11", "x_va"])
    project("x", k["woxT"], t["oT"], 1, ["x_oc"])
    dve("x_y", lambda e: e.tensor_tensor(t["xa"][:], ps[:, 1, 0:D], t["xb"][:], ALU.add), "x_pr1", "m_xb")

    layer_norm_only = [("g_st", lambda e: e.bn_stats(t["stat"][:, 0:6], t["xa"][:]), ["x_y"], 256),
                       ("g_mv", lambda e: e.bn_aggr(t["sv"][:, 0:2], t["stat"][:, 0:6]), ["g_st"], 8),
                       ("g_ve", lambda e: e.tensor_scalar(t["sv"][:, 2:3], t["sv"][:, 1:2], LN_EPS, None, ALU.add), ["g_mv"], 8)]
    for name, emit, after, n in layer_norm_only:
        dve(name, emit, *after, n=n, plain=n == 8)
    ch.step(POOL, "g_rs", lambda e, _: e.tensor_tensor(t["sv"][:, 3:4], t["sv"][:, 2:3], k["neg_half"][:], ALU.pow),
            ["g_ve"], cost=1.0)
    dve("g_xn", lambda e: e.tensor_scalar(t["xn"][:], t["xa"][:], t["sv"][:, 0:1], t["sv"][:, 3:4], ALU.subtract, ALU.mult),
        "g_rs")
    qs = t["qs"]
    dve("g_am", lambda e: e.tensor_reduce(qs[:, 0:1], t["xn"][:], AX.X, ALU.max, apply_absolute_value=True), "g_xn")
    dve("g_cl", lambda e: e.tensor_scalar(qs[:, 0:1], qs[:, 0:1], 1e-5, None, ALU.max), "g_am", n=8)
    dve("g_rc", lambda e: e.reciprocal(qs[:, 1:2], qs[:, 0:1]), "g_cl", n=8)
    dve("g_sc", lambda e: e.tensor_scalar(qs[:, 2:3], qs[:, 1:2], 127.0, None, ALU.mult), "g_rc", n=8)
    dve("g_bk", lambda e: e.tensor_scalar(qs[:, 3:4], qs[:, 0:1], k["w1t_back"][:, 0:1], None, ALU.mult), "g_cl", n=8)
    dve("g_q1", lambda e: e.tensor_scalar(t["xq"][:], t["xn"][:], qs[:, 2:3], ROUND, ALU.mult, ALU.add), "g_sc")
    dve("g_q2", lambda e: e.tensor_scalar(t["xqb"][:], t["xq"][:], -ROUND, None, ALU.add), "g_q1")
    dve("g_dg", lambda e: e.tensor_scalar(t["dg"][:], k["ident"][:], qs[:, 3:4], None, ALU.mult), "g_bk", n=128)
    mm("g_bb", ps[:, 0, 0:T], k["ones"][:], t["dg"][:], "g_dg", "x_o")
    act("g_bc", lambda e: e.copy(t["back"][:], ps[:, 0, 0:T]), "g_bb", n=128)
    half = ps[:, 3, :].bitcast(BF16)
    for j in range(KT):
        flip(f"g_T{j}", half[:, T * j:T * j + T], t["xqb"][:, 128 * j:128 * j + 128], "g_q2", "x_o", ident=k["ident_bf"])
    act("g_xqT", lambda e: e.copy(t["xqT"][:], half[:, 0:D].rearrange("p (k t) -> p k t", k=KT)), "g_T1")
    for m in range(HT):
        for j in range(KT):
            mm(f"g_h{m}{j}", ps[:, 1 + m // 4, T * (m % 4):T * (m % 4) + T],
               k["w1t"][:, HID * j + 128 * m:HID * j + 128 * m + 128], t["xqT"][:, j, :], "g_xqT", "x_y",
               start=(j == 0), stop=(j == KT - 1), passes=1)
    cv, cwt = t["cv"], k["conv_w"]
    for q in range(2):
        m0 = 4 * q
        dve(f"g_hp{q}", lambda e, q=q, m0=m0: e.tensor_tensor(
            t["hp"][:, m0:m0 + 4, 1:1 + T], ps[:, 1 + q, :].rearrange("p (m t) -> p m t", t=T),
            spread(t["back"][:], 1, 4), ALU.mult), f"g_h{m0 + 3}1", "g_bc", n=512)
        for m in range(m0, m0 + 4):
            act(f"g_c{m}", lambda e, m=m: e.activation(cv[:, m, :], t["hp"][:, m, 1:1 + T], ACT.Identity,
                                                       scale=cwt[:, m, 1:2], bias=k["conv_b"][:, m:m + 1]), f"g_hp{q}", n=250)
        for tap, sh in ((0, 0), (2, 2)):
            for m in range(m0, m0 + 4):
                dve(f"g_t{tap}{m}", lambda e, m=m, tap=tap, sh=sh: e.scalar_tensor_tensor(
                    out=cv[:, m, :], in0=t["hp"][:, m, sh:sh + T], scalar=cwt[:, m, tap:tap + 1], in1=cv[:, m, :],
                    op0=ALU.mult, op1=ALU.add), f"g_c{m}" if tap == 0 else f"g_t0{m}", n=190)
    for q in range(2):
        v = slice(4 * q, 4 * q + 4)
        act(f"g_th{q}", lambda e, v=v: e.activation(t["hid"][:, v, :], cv[:, v, :], ACT.Tanh, scale=0.5), f"g_t2{4 * q + 3}", n=512)
        dve(f"g_si{q}", lambda e, v=v: e.scalar_tensor_tensor(
            out=t["hid"][:, v, :].rearrange("p m t -> p (m t)"), in0=t["hid"][:, v, :].rearrange("p m t -> p (m t)"), scalar=1.0,
            in1=cv[:, v, :].rearrange("p m t -> p (m t)"), op0=ALU.add, op1=ALU.mult), f"g_th{q}", n=512)
        for m in range(4 * q, 4 * q + 4):
            flip(f"g_hT{m}", ps[:, 1 + q, T * (m - 4 * q):T * (m - 4 * q) + T], t["hid"][:, m, :], f"g_si{q}")
    tok = ps[:, 1:3, :].rearrange("p a b -> p (a b)")
    dve("g_am2", lambda e: e.tensor_reduce(qs[:, 4:5], tok, AX.X, ALU.max, apply_absolute_value=True), "g_hT7", n=1024)
    dve("g_cl2", lambda e: e.tensor_scalar(qs[:, 4:5], qs[:, 4:5], 2e-5, None, ALU.max), "g_am2", n=8)
    dve("g_rc2", lambda e: e.reciprocal(qs[:, 5:6], qs[:, 4:5]), "g_cl2", n=8)
    dve("g_sc2", lambda e: e.tensor_scalar(qs[:, 6:7], qs[:, 5:6], 127.0, None, ALU.mult), "g_rc2", n=8)
    dve("g_bk2", lambda e: e.tensor_scalar(qs[:, 7:8], qs[:, 4:5], k["w2t_back"][:, 0:1], None, ALU.mult), "g_cl2", n=8)
    flat = cv[:].rearrange("p m t -> p (m t)")
    dve("g_r1", lambda e: e.tensor_scalar(flat, tok, qs[:, 6:7], ROUND, ALU.mult, ALU.add), "g_sc2", "g_si1", n=1024)
    dve("g_r2", lambda e: e.tensor_scalar(t["hqb"][:], flat, -ROUND, None, ALU.add), "g_r1", n=512)
    for m in range(HT):
        flip(f"g_qT{m}", half[:, T * m:T * m + T], t["hqb"][:, 128 * m:128 * m + 128], "g_r2", "g_xqT", ident=k["ident_bf"])
    act("g_qc", lambda e: e.copy(t["hqT"][:], half[:, 0:HID].rearrange("p (m t) -> p m t", t=T)), "g_qT7", n=1024)
    for m in range(HT):
        mm(f"g_o{m}", ps[:, 0, 0:D], t["hqT"][:, m, :], k["w2t"][:, D * m:D * m + D], "g_qc", start=(m == 0), stop=(m == HT - 1),
           passes=1)
    dve("y", lambda e: e.scalar_tensor_tensor(out=t["out"][:], in0=ps[:, 0, 0:D], scalar=qs[:, 7:8], in1=t["xa"][:],
                                              op0=ALU.mult, op1=ALU.add), "g_o7", "g_bk2", "b_xb", ("before", "store"))
    ch.step(ACTE, "store", lambda e, turn: e.dma_start(dram["out"](turn), t["out"][:]), ["y"], cost=0.1, count="store")


def decoder(nc, inp, x, ctx_in, mask, out):
    with ExitStack() as ctx:
        def opener(stack, side="left"):
            def sb(name, shape, dt=F32):
                return stack.enter_context(nc.sbuf_tensor(name, shape, dt, side=side))
            return sb

        nc.disable_value_cache = True
        sb = opener(ctx)
        ps = ctx.enter_context(nc.psum_tensor("banks", [128, 8, 512], F32))
        k = {}
        setup = Chain("setup")
        with ExitStack() as scratch:
            setup_steps(nc, setup, sb, opener(scratch, "right"), ps, inp, k)
        setup.open(nc, ctx)

        chains, tiles = [], []
        for c in range(NCHAIN):
            ch = Chain(f"chain{c}")
            t = buffers(nc, sb, ch.label)
            by_turn = {name: ap.rearrange("(n c) t d -> n c t d", c=NCHAIN) for name, ap in
                       (("x", x), ("ctx", ctx_in), ("out", out))}
            mask_t = mask.rearrange("(n c) t -> n c t", c=NCHAIN)
            dram = {"out": lambda turn, c=c: by_turn["out"][turn, c]}
            ch.step(SP, "x_in", lambda e, turn, c=c, t=t: e.dma_start(t["x_in"][:], by_turn["x"][turn, c]),
                    [("before", "a_st"), ("before", "a_xn"), ("before", "a_xb")], count="x_in")
            ch.step(SP, "mask_r", lambda e, turn, c=c, t=t: e.dma_start(
                t["mask_r"][0:128:32, :], mask_t[turn, c].partition_broadcast(4)), [("before", "mask_bf")], count="mask_r")
            ch.step(SP, "mask_c", lambda e, turn, c=c, t=t: e.dma_start(
                t["mask_c"][:], mask_t[turn, c].rearrange("(t a) -> t a", a=1)), [("before", "b_y"), ("before", "b_xb1")], count="mask_c")
            ch.step(SP, "ctx", lambda e, turn, c=c, t=t: e.dma_start(t["ctx"][:], by_turn["ctx"][turn, c]),
                    [("before", "b_va"), ("before", "c_T1")], count="ctx")
            sequence_steps(ch, t, ps[:, 4 * c:4 * c + 4, :], k, dram)
            ch.open(nc, ctx)
            chains.append(ch)
            tiles.append(t)
        clear = ctx.enter_context(nc.semaphore("cleared"))
        unread = ctx.enter_context(nc.semaphore("unread"))

        lists = []
        for ch in chains:
            steps = [s for s in ch.steps if s.engine != SP]
            cut = next(i for i, s in enumerate(steps) if s.name == "n_st")
            lists.append(([(ch, s, 0) for s in steps[:cut]], [(ch, s, 0) for s in steps[cut:]]))
        (a1, a2), (b1, b2) = lists
        later = [(c, s, 1) for c, s, _ in b1]
        order_head = interleave([b1])
        order_turn = interleave([a1 + a2, b2 + later])
        order_tail = interleave([a1 + a2, b2])
        block = ctx.enter_context(nc.Block())

        def main(engine, name):
            for key, sem in setup.sems.items():
                engine.wait_ge(sem, setup.total[key] * (1 if key in (PE, DVE, ACTE, POOL) else 16))
            if name == POOL:
                for t in tiles:
                    for tile in ("kp", "vp", "hp", "mask_r"):
                        engine.memset(t[tile][:], 0.0).then_inc(clear, 1)
                    engine.memset(t["va"][:], 1.0).then_inc(clear, 1)
            engine.wait_ge(clear, 5 * NCHAIN)
            if name == SP:
                for ch in chains:
                    for key in ("x_in", "mask_r", "mask_c", "ctx"):
                        engine.sem_inc(ch.sems[key], 16)
                with engine.Fori(0, TURNS) as turn:
                    known = {}
                    at = {ch.label: turn for ch in chains}
                    for step in ("x_in", "mask_r", "mask_c", "ctx"):
                        run_queue(engine, [(ch, ch.by_name[step], 0) for ch in chains], at, known, unread=unread)
                return
            for ch in chains:
                if name in ch.total:
                    engine.sem_inc(ch.sems[name], ch.total[name])
                if name == ACTE:
                    engine.sem_inc(ch.sems["store"], 16)
            run_queue(engine, order_head[name], {"chain1": 0}, {}, unread=unread)
            with engine.Fori(0, TURNS - 1) as turn:
                run_queue(engine, order_turn[name], {"chain0": turn, "chain1": turn}, {}, unread=unread)
            run_queue(engine, order_tail[name], {"chain0": TURNS - 1, "chain1": TURNS - 1}, {}, unread=unread)
            if name == ACTE:
                for ch in chains:
                    engine.wait_ge(ch.sems["store"], 16 + 16 * TURNS)

        def program(name):
            def run(engine):
                if name == POOL:
                    pass
                run_queue(engine, [(setup, s, 0) for s in setup.steps if s.engine == name], {"setup": 0}, {}, False)
                main(engine, name)
            return run

        for name in (SP, POOL, DVE, ACTE, PE):
            {SP: block.sync, POOL: block.gpsimd, DVE: block.vector, ACTE: block.scalar, PE: block.tensor}[name](program(name))


def shape_constants():
    p = np.arange(128)
    f = np.float32
    expand = np.zeros((WIN, H, WIN, KT, 128), f)
    for w in range(WIN):
        for j in range(KT):
            for r in range(128):
                expand[w, 8 * j + r // DH, w, j, r] = 1
    s = 32 * (p[:, None] // 32) + np.arange(32)[None, :]
    return {
        "ident": np.eye(128, dtype=f),
        "parity": np.stack([(p % 32 < 16), (p % 32 >= 16)], 1).astype(f),
        "head_ones": (p[:, None] // DH == np.arange(8)[None, :]).astype(f),
        "expand": expand.reshape(WIN * H, WIN * KT * 128),
        "causal": np.where(p[None, :] > p[:, None], f(CAUSAL), f(0)),
        "rel": (p[None, None, :] - s[:, :, None]).astype(f).reshape(128, 32 * 128),
        "pos": np.tile(p.astype(f), (128, 1)),
        "pos7": np.tile(np.linspace(0.0, 1.0, WIN, dtype=f), (H, 1)),
        "diag16": np.tile(np.eye(H, dtype=f)[:, None, :], (1, WIN, 1)),
    }


def kernel(**inputs):
    import concourse.bacc as bacc
    from concourse.bass_utils import run_bass_kernel_spmd

    v = {name: np.asarray(a) for name, a in inputs.items()}
    w1 = v["L0_ffn_w1"]
    qkv_b = v["L1_attn_bqkv"]
    conv_w = v["L1_ffn_conv_w"].reshape(HT, 128, 3)

    def cols(a):
        return a.reshape(-1, 128).T

    laid = {
        "wqkv0T": np.concatenate([v["L0_attn_wq"].T, v["L0_attn_wk"].T, v["L0_attn_wv"].T], 1),
        "wo0T": v["L0_attn_wo"].T, "bo0": v["L0_attn_bo"],
        "cw1": v["L0_attn_cw1"].reshape(H, 32), "cb1": v["L0_attn_cb1"], "cw2": v["L0_attn_cw2"],
        "cb2": v["L0_attn_cb2"], "cw3": v["L0_attn_cw3"].reshape(H, 32), "cb3": v["L0_attn_cb3"],
        "wpT": v["L0_xattn_Wp"].T, "bp": v["L0_xattn_bp"],
        "slot_init": v["L0_ffn_slot_init"], "slot_scale": v["L0_ffn_slot_scale"],
        "w1aT": w1[:, :D].T, "w1bT": w1[:, D:].T, "b1f": cols(v["L0_ffn_b1"]), "w2fT": v["L0_ffn_w2"].T, "b2f": v["L0_ffn_b2"],
        "wihT": v["L0_ffn_gru_wih"].T, "whhT": v["L0_ffn_gru_whh"].T, "bih": v["L0_ffn_gru_bih"], "bhh": v["L0_ffn_gru_bhh"],
        "wvf": v["L0_ffn_wv"], "bvf": cols(v["L0_ffn_bv"]), "wofT": v["L0_ffn_wo"].T, "bof": v["L0_ffn_bo"], "tau": v["L0_ffn_tau"],
        "wqkv1": v["L1_attn_Wqkv"], "bq1": cols(qkv_b[:D]), "bk1": cols(qkv_b[D:2 * D]), "bv1": qkv_b[2 * D:],
        "wproj": v["L1_attn_Wproj"], "bproj": v["L1_attn_bproj"],
        "fw1": v["L1_attn_w1"].reshape(32, 1), "fb1": v["L1_attn_b1"].reshape(32, 1), "fw2": v["L1_attn_w2"],
        "fb2": v["L1_attn_b2"], "c_param": v["L1_attn_c_param"].reshape(1), "l_mult": v["L1_attn_L_multiplier"].reshape(1),
        "wqkvxT": np.concatenate([v["L1_xattn_Wq"].T, v["L1_xattn_Wk"].T, v["L1_xattn_Wv"].T], 1),
        "bqx": cols(v["L1_xattn_bq"]), "bkx": cols(v["L1_xattn_bk"]), "bvx": v["L1_xattn_bv"],
        "woxT": v["L1_xattn_Wo"].T, "box": v["L1_xattn_bo"],
        "w1t": v["L1_ffn_w1"].T, "w2t": v["L1_ffn_w2"].T,
        "conv_w": np.transpose(conv_w, (1, 0, 2)), "conv_b": v["L1_ffn_conv_b"].reshape(HT, 128).T,
        **shape_constants(),
    }
    nc = bacc.Bacc("TRN2", target_bir_lowering=False, num_devices=1)
    arrays, inp = {}, {}

    def given(name, a):
        arrays[name] = np.ascontiguousarray(a)
        return nc.dram_tensor(name, arrays[name].shape, F32, kind="ExternalInput").ap()

    for name, a in laid.items():
        inp[name] = given("in_" + name, a)
    x, c, m = given("in_x", v["x"]), given("in_ctx", v["ctx_1024"]), given("in_mask", v["mask_BxS2_fk1"])
    out = nc.dram_tensor("out", (NSEQ, T, D), F32, kind="ExternalOutput").ap()
    decoder(nc, inp, x, c, m, out)
    return run_bass_kernel_spmd(nc, [arrays], core_ids=[0]).results[0]["out"]
```

```python
from contextlib import ExitStack

import numpy as np
import concourse.bass as bass
from concourse import mybir

F32 = mybir.dt.float32
BF16 = mybir.dt.bfloat16
ACT = mybir.ActivationFunctionType
ALU = mybir.AluOpType
AX = mybir.AxisListType

NSEQ, T, D = 64, 128, 256
H, DH = 16, 16
KT = D // 128
WIN, PAD = 7, 3
SLOTS, GATES = 64, 768
HID = 1024
HT = HID // 128
NCHAIN = 4
TURNS = NSEQ // NCHAIN
LN_EPS = 1e-5
ROUND = 12582912.0
MASKED = 1e9
CAUSAL = 1e30
GROUPS = 4
PER = H // GROUPS
VC = 2 * DH

PE, DVE, ACTE, POOL, SP = "tensor", "vector", "scalar", "gpsimd", "sync"
HOP = {PE: 0.26, DVE: 0.16, ACTE: 0.26, POOL: 0.16, SP: 2.0}
WINDOW, BUSY = 3.4, 0.8
WARM = 0.22


class Step:
    def __init__(self, engine, name, emit, after, cost, count):
        self.engine, self.name, self.emit, self.after, self.cost = engine, name, emit, after, cost
        self.count = count
        self.inc = 1 if count in (engine, None) else 16
        self.place = None
        self.plain = False


class Chain:

    def __init__(self, label):
        self.label, self.steps, self.by_name, self.total = label, [], {}, {}
        self.vacant = {}

    def step(self, engine, name, emit, after=(), cost=0.3, count=None, plain=False):
        assert name not in self.by_name, name
        s = Step(engine, name, emit, list(after), cost, count or engine)
        self.total[s.count] = self.total.get(s.count, 0) + 1
        s.place = self.total[s.count]
        s.plain = plain
        self.steps.append(s)
        self.by_name[name] = s
        return name

    def meanwhile(self, name, emit, after):
        s = Step(PE, "warm_" + name, emit, list(after), WARM, None)
        self.vacant[name] = s

    def open(self, nc, ctx):
        self.sems = {k: ctx.enter_context(nc.semaphore(f"{self.label}_{k}_done")) for k in self.total}

    def value(self, name, start_ahead):
        before = isinstance(name, tuple)
        s = self.by_name[name[1] if before else name]
        n = self.total[s.count]
        at = s.place * s.inc + (n * s.inc if start_ahead else 0) - (n * s.inc if before else 0)
        return self.sems[s.count], n * s.inc, at, (s.count, before, s.place)


def run_queue(engine, queue, turn, start_ahead=True, unread=None):
    bases, known = {}, {}
    for chain, s, shift in queue:
        need = {}
        for name in s.after:
            sem, per_sequence, value, (count, before, place) = chain.value(name, start_ahead)
            value += shift * per_sequence
            static = shift * chain.total[count] + place - (chain.total[count] if before else 0)
            if need.get(count, (None, None, None, -10**9))[3] < static:
                need[count] = (sem, per_sequence, value, static)
        for count, (sem, per_sequence, value, static) in need.items():
            if known.get((chain.label, count), -10**9) >= static:
                continue
            known[(chain.label, count)] = static
            if not isinstance(turn, int):
                if (chain.label, count) not in bases:
                    bases[chain.label, count] = engine.snap(turn * per_sequence)
                engine.wait_ge(sem, bases[chain.label, count] + value)
            else:
                engine.wait_ge(sem, turn * per_sequence + value)
        if need and s.plain and start_ahead:
            engine.sem_inc(unread, 1)
        done = s.emit(engine, turn + shift)
        if s.count:
            done.then_inc(chain.sems[s.count], s.inc)


def to_the_end(part):
    readers, path, same_engine = {}, {}, {}
    for _, s, shift in part:
        for name in s.after:
            readers.setdefault((name, shift), []).append((s.name, shift))
    for _, s, shift in reversed(part):
        after = [path[r] + HOP[s.engine] for r in readers.get((s.name, shift), ()) if r in path]
        path[s.name, shift] = same_engine[s.engine] = s.cost + max(after + [same_engine.get(s.engine, 0.0)])
    return path


def interleave(parts):
    engines = (PE, DVE, ACTE, POOL)
    lanes = {e: [[(c, s, sh) for c, s, sh in part if s.engine == e] for part in parts] for e in engines}
    paths = [to_the_end(part) for part in parts]
    free = dict.fromkeys(engines, 0.0)
    done = [dict() for _ in parts]
    pending = [set((s.name, sh) for _, s, sh in part) for part in parts]
    order = {e: [] for e in engines}
    busy = []
    for _ in range(sum(len(part) for part in parts)):
        ready = []
        for e in engines:
            for k, lane in enumerate(lanes[e]):
                if not lane:
                    continue
                chain, s, shift = lane[0]
                deps = [(n[1], shift - 1) if isinstance(n, tuple) else (n, shift) for n in s.after]
                if any(n in pending[k] for n in deps):
                    continue
                start = max([free[e]] + [done[k][n] + HOP[chain.by_name[n[0]].engine] for n in deps if n in done[k]])
                ready.append((start, engines.index(e), -paths[k][s.name, shift], k))
        start, at, _, k = min(ready)
        e = engines[at]
        while e == PE and free[PE] + WARM < start and sum(
                max(0.0, min(b, start) - max(a, start - WINDOW)) for a, b in busy) < BUSY * WINDOW:
            begin = []
            for c, lane in enumerate(lanes[PE]):
                if lane and lane[0][1].name in lane[0][0].vacant:
                    chain, shift = lane[0][0], lane[0][2]
                    s = chain.vacant[lane[0][1].name]
                    deps = [(n[1], shift - 1) if isinstance(n, tuple) else (n, shift) for n in s.after]
                    if not any(n in pending[c] for n in deps):
                        begin.append((max([free[PE]] + [done[c][n] + HOP[chain.by_name[n[0]].engine] for n in deps
                                                        if n in done[c]]), c, (chain, s, shift)))
            if not begin or min(begin)[0] + WARM > start:
                break
            free[PE] = min(begin)[0] + WARM
            busy = busy[-40:] + [(min(begin)[0], free[PE])]
            order[PE].append(min(begin)[2])
        item = lanes[e][k].pop(0)
        free[e] = start + item[1].cost
        if e == PE:
            busy = busy[-40:] + [(start, free[PE])]
        done[k][item[1].name, item[2]] = free[e]
        pending[k].discard((item[1].name, item[2]))
        order[e].append(item)
    return order


def spread(ap, dim, n):
    ap = ap.unsqueeze(dim)
    shape = list(ap.shape)
    shape[dim] = n
    return ap.broadcast_to(shape)


def windows(tile, w0, n):
    ap = tile[:, :, w0:w0 + T]
    return bass.AP(ap.tensor, ap.offset, [list(ap.ap[0]), [1, n], [T + 2 * PAD, KT], [1, T]])


def setup_steps(nc, st, sb, tmp, ps, inp, k):

    def load(name, dst, src):
        st.step(SP, name, lambda e, _: e.dma_start(dst, src), count=name)
        return name

    def dve(name, emit, *after):
        return st.step(DVE, name, lambda e, _: emit(e), after)

    def act(name, emit, *after):
        return st.step(ACTE, name, lambda e, _: emit(e), after)

    def pe(name, emit, *after):
        return st.step(PE, name, lambda e, _: emit(e), after)

    def tiles(ap):
        return ap.rearrange("(k p) n -> p k n", p=128)

    def rows(ap, p=128):
        return ap.partition_broadcast(p)

    for name, shape in (("wqkv0T", [128, KT, 3 * D]), ("wo0T", [128, KT, D]), ("wpT", [128, KT, D]),
                        ("w1aT", [128, KT, 128]), ("w1bT", [128, KT, 128]), ("wihT", [128, KT, GATES]),
                        ("wqkv1", [128, KT, 3 * D]), ("wproj", [128, KT, D]), ("wqkvxT", [128, KT, 3 * D]),
                        ("woxT", [128, KT, D])):
        k[name] = (tmp if name == "w1bT" else sb)(name, shape)
        load("ld_" + name, k[name][:], tiles(inp[name]))
    for name, shape in (("w2fT", [128, SLOTS]), ("ident", [128, 128]), ("parity", [128, 2]),
                        ("head_sum", [128, KT * 32]), ("expand", [96, 4 * 128])):
        k[name] = sb(name, shape)
        load("ld_" + name, k[name][:], inp[name])
    for name, src, n in (("bo0_r", "bo0", D), ("bp_r", "bp", D), ("bof_r", "bof", D), ("bproj_r", "bproj", D),
                         ("box_r", "box", D), ("bv1_r", "bv1", D), ("bvx_r", "bvx", D), ("b2f_r", "b2f", SLOTS)):
        k[name] = sb(name, [128, n])
        load("ld_" + name, k[name][:], rows(inp[src]))

    k["expand_bf"] = sb("expand_bf", [96, 4, 128], BF16)
    dve("expand_bf", lambda e: e.tensor_copy(k["expand_bf"][:].rearrange("p a b -> p (a b)"), k["expand"][:]), "ld_expand")
    k["ident_bf"] = sb("ident_bf", [128, 128], BF16)
    dve("ident_bf", lambda e: e.tensor_copy(k["ident_bf"][:], k["ident"][:]), "ld_ident")
    k["ones"] = sb("ones", [128, 128])
    dve("ones", lambda e: e.memset(k["ones"][:], 1.0))
    k["ones_bf"] = sb("ones_bf", [128, 128], BF16)
    dve("ones_bf", lambda e: e.memset(k["ones_bf"][:], 1.0))
    k["neg_half"] = sb("neg_half", [128, 1])
    dve("neg_half", lambda e: e.memset(k["neg_half"][:], -0.5))

    for tag in ("1", "x"):
        q, b = tmp("bq_c" + tag, [128, KT]), tmp("bk_c" + tag, [128, KT])
        k["bq" + tag] = sb("bq" + tag, [128, KT])
        k["bk" + tag] = sb("bk" + tag, [128, KT, 2])
        load("ld_bq" + tag, q[:], inp["bq" + tag])
        load("ld_bk" + tag, b[:], inp["bk" + tag])
        dve("bq" + tag, lambda e, q=q, tag=tag: e.tensor_scalar(k["bq" + tag][:], q[:], -0.25, None, ALU.mult), "ld_bq" + tag)
        for o in range(2):
            dve(f"bk{tag}{o}", lambda e, b=b, tag=tag, o=o: e.tensor_scalar(
                k["bk" + tag][:, :, o], b[:], k["parity"][:, o:o + 1], None, ALU.mult), "ld_bk" + tag, "ld_parity")

    rel, pos, w1c, b1w = tmp("rel", [128, 32, T]), tmp("pos", [128, T]), tmp("fw1", [128, 1]), tmp("fb1", [128, 1])
    w2c, b2r, cau = tmp("fw2", [128, H]), tmp("fb2_r", [128, H]), tmp("causal", [128, T])
    cpar, lmul = tmp("cpar", [128, 1]), tmp("lmul", [128, 1])
    load("ld_rel", rel[:].rearrange("p a b -> p (a b)"), inp["rel"])
    load("ld_pos", pos[:], inp["pos"])
    load("ld_causal", cau[:], inp["causal"])
    load("ld_cpar", cpar[:], rows(inp["c_param"]))
    load("ld_lmul", lmul[:], rows(inp["l_mult"]))
    load("ld_fb2", b2r[:], rows(inp["fb2"]))
    for g in range(4):
        load(f"ld_fw1{g}", w1c[32 * g:32 * g + 32, :], inp["fw1"])
        load(f"ld_fb1{g}", b1w[32 * g:32 * g + 32, :], inp["fb1"])
        load(f"ld_fw2{g}", w2c[32 * g:32 * g + 32, :], inp["fw2"])
    act("fire1", lambda e: e.activation(rel[:], rel[:], ACT.Abs, scale=cpar[:, 0:1]), "ld_rel", "ld_cpar")
    act("fire2", lambda e: e.activation(lmul[:], lmul[:], ACT.Abs, scale=512.0), "ld_lmul")
    dve("fire3", lambda e: e.tensor_scalar(pos[:], pos[:], lmul[:, 0:1], None, ALU.max), "fire2", "ld_pos")
    act("fire4", lambda e: e.activation(pos[:], pos[:], ACT.Abs, scale=cpar[:, 0:1]), "fire3")
    act("fire5", lambda e: e.activation(pos[:], pos[:], ACT.Ln, bias=1.0), "fire4")
    act("fire6", lambda e: e.activation(rel[:], rel[:], ACT.Ln, bias=1.0), "fire1")
    dve("fire7", lambda e: e.tensor_scalar(pos[:], pos[:], 1e-6, None, ALU.add), "fire5")
    dve("fire8", lambda e: e.reciprocal(pos[:], pos[:]), "fire7")
    dve("fire9", lambda e: e.tensor_tensor(rel[:], rel[:], spread(pos[:], 1, 32), ALU.mult), "fire6", "fire8")
    act("fire10", lambda e: e.activation(rel[:], rel[:], ACT.Relu, scale=w1c[:, 0:1], bias=b1w[:, 0:1]),
        "fire9", *[f"ld_fw1{g}" for g in range(4)], *[f"ld_fb1{g}" for g in range(4)])
    wd = tmp("fire_w", [128, 4, H])
    dve("fire_w0", lambda e: e.memset(wd[:], 0.0))
    for g in range(4):
        r = slice(32 * g, 32 * g + 32)
        dve(f"fire_w{g + 1}", lambda e, g=g, r=r: e.tensor_scalar(wd[r, g, :], w2c[r, :], -1.0, None, ALU.mult),
            f"ld_fw2{g}", "fire_w0")
    dve("fire12", lambda e: e.tensor_scalar(b2r[:], b2r[:], -1.0, None, ALU.mult), "ld_fb2")
    k["pos_bias"] = sb("pos_bias", [128, GROUPS, KT, 2, T])
    fb = tmp("fire_b", [128, 4, 32, H])
    for s in range(32):
        pe(f"fire_mm{s}", lambda e, s=s: e.matmul(ps[:, s // 8, 64 * (s % 8):64 * (s % 8) + 64], rel[:, s, :],
                                                  wd[:].rearrange("p g h -> p (g h)"), start=True, stop=True), "fire10", "fire_w4")
    for b in range(4):
        dve(f"fire_b{b}", lambda e, b=b: e.tensor_tensor(
            fb[:, :, 8 * b:8 * b + 8, :], ps[:, b, :].rearrange("p (s g h) -> p g s h", s=8, g=4),
            spread(spread(b2r[:], 1, 8), 1, 4), ALU.add), f"fire_mm{8 * b + 7}", "fire12")
    for g in range(4):
        for j in range(KT):
            for q in range(GROUPS):
                dve(f"pos_bias{g}{j}{q}", lambda e, g=g, j=j, q=q: e.tensor_tensor(
                    k["pos_bias"][:, q, j, :, 32 * g:32 * g + 32],
                    fb[:, g, :, 8 * j + 2 * q:8 * j + 2 * q + 2].rearrange("p s o -> p o s"),
                    spread(cau[:, 32 * g:32 * g + 32], 1, 2), ALU.add), "fire_b3", "ld_causal")

    c = {}
    for name, shape in (("cw1", [H, 32]), ("cb1", [H, 32]), ("cw2", [H, 32, 32]), ("cb2", [H, 32]),
                        ("cw3", [H, 32]), ("cb3", [H, 1]), ("pos7", [H, WIN]), ("diag16", [H, WIN, H])):
        c[name] = tmp("c_" + name, shape)
        load("ld_" + name, c[name][:], inp[name])
    h1, h2, cw = tmp("conn_h1", [H, WIN, 32]), tmp("conn_h2", [H, WIN, 32]), tmp("conn_w", [H, WIN])
    z, cs, dg = tmp("conn_z", [H, WIN, 32, 32]), tmp("conn_s", [H, 1]), tmp("conn_d", [H, WIN, H])
    k["conn"] = sb("conn", [128, WIN * H])
    dve("conn1", lambda e: e.tensor_tensor(h1[:], spread(c["pos7"][:], 2, 32), spread(c["cw1"][:], 1, WIN), ALU.mult),
        "ld_pos7", "ld_cw1")
    dve("conn2", lambda e: e.tensor_tensor(h1[:], h1[:], spread(c["cb1"][:], 1, WIN), ALU.add), "conn1", "ld_cb1")
    act("conn3", lambda e: e.activation(h1[:], h1[:], ACT.Gelu), "conn2")
    dve("conn4", lambda e: e.tensor_tensor(z[:], spread(h1[:], 2, 32), spread(c["cw2"][:], 1, WIN), ALU.mult),
        "conn3", "ld_cw2")
    dve("conn5", lambda e: e.tensor_reduce(h2[:], z[:], AX.X, ALU.add), "conn4")
    dve("conn6", lambda e: e.tensor_tensor(h2[:], h2[:], spread(c["cb2"][:], 1, WIN), ALU.add), "conn5", "ld_cb2")
    act("conn7", lambda e: e.activation(h2[:], h2[:], ACT.Gelu), "conn6")
    dve("conn8", lambda e: e.tensor_tensor(h2[:], h2[:], spread(c["cw3"][:], 1, WIN), ALU.mult), "conn7", "ld_cw3")
    dve("conn9", lambda e: e.tensor_reduce(cw[:], h2[:], AX.X, ALU.add), "conn8")
    dve("conn10", lambda e: e.tensor_scalar(cw[:], cw[:], c["cb3"][:, 0:1], None, ALU.add), "conn9", "ld_cb3")
    dve("conn11", lambda e: e.tensor_reduce(cs[:], cw[:], AX.X, ALU.max, negate=True), "conn10")
    act("conn12", lambda e: e.activation(cw[:], cw[:], ACT.Exp, bias=cs[:, 0:1]), "conn11")
    dve("conn13", lambda e: e.tensor_reduce(cs[:], cw[:], AX.X, ALU.add), "conn12")
    dve("conn14", lambda e: e.reciprocal(cs[:], cs[:]), "conn13")
    dve("conn15", lambda e: e.tensor_scalar(cw[:], cw[:], cs[:, 0:1], None, ALU.mult), "conn14")
    dve("conn16", lambda e: e.tensor_tensor(dg[:], spread(cw[:], 2, H), c["diag16"][:], ALU.mult),
        "conn15", "ld_diag16")
    pe("conn17", lambda e: e.matmul(ps[:, 0, 0:WIN * H], k["ones"][0:H, :], dg[:].rearrange("p a b -> p (a b)"),
                                    start=True, stop=True), "conn16", "ones", "fire_b3")
    dve("conn", lambda e: e.tensor_copy(k["conn"][:], ps[:, 0, 0:WIN * H]), "conn17")

    slot, scale = tmp("slot_init", [SLOTS, D]), tmp("slot_scale", [SLOTS, 1])
    load("ld_slot", slot[:], inp["slot_init"])
    load("ld_slot_scale", scale[:], inp["slot_scale"])
    whh, bhh, bih = tmp("whhT", [128, KT, GATES]), tmp("bhh_r", [SLOTS, GATES]), tmp("bih_r", [SLOTS, GATES])
    load("ld_whh", whh[:], tiles(inp["whhT"]))
    load("ld_bhh", bhh[:], rows(inp["bhh"], SLOTS))
    load("ld_bih", bih[:], rows(inp["bih"], SLOTS))
    b1c, meanT, slotT = tmp("b1_c", [128, 1]), tmp("slot_meanT", [128, KT]), tmp("slotT", [128, KT, SLOTS])
    load("ld_b1f", b1c[:], inp["b1f"])
    k["slots"] = sb("slots", [SLOTS, D])
    dve("slots", lambda e: e.tensor_scalar(k["slots"][:], slot[:], scale[:, 0:1], None, ALU.mult), "ld_slot", "ld_slot_scale")
    for j in range(KT):
        s_j = k["slots"][:, 128 * j:128 * j + 128]
        pe(f"slot_mean{j}", lambda e, s_j=s_j, j=j: e.matmul(ps[:, 1, j:j + 1], s_j, k["ones"][0:SLOTS, 0:1],
                                                             start=True, stop=True), "slots", "ones", "fire_b3")
        pe(f"slotT{j}", lambda e, s_j=s_j, j=j: e.transpose(ps[:, 2, SLOTS * j:SLOTS * j + SLOTS], s_j,
                                                            k["ident"][0:SLOTS, 0:SLOTS]), "slots", "ld_ident")
    dve("slot_mean", lambda e: e.tensor_scalar(meanT[:], ps[:, 1, 0:KT], 1.0 / SLOTS, None, ALU.mult), "slot_mean1")
    dve("slotT", lambda e: e.tensor_copy(slotT[:], ps[:, 2, 0:KT * SLOTS].rearrange("p (k s) -> p k s", k=KT)), "slotT1")
    k["hid_bias"] = sb("hid_bias", [128, 1])
    for j in range(KT):
        pe(f"hid_bias{j}", lambda e, j=j: e.matmul(ps[:, 3, 0:1], k["w1bT"][:, j, :], meanT[:, j:j + 1],
                                                   start=(j == 0), stop=(j == KT - 1)), "slot_mean", "ld_w1bT")
    dve("hid_bias", lambda e: e.tensor_tensor(k["hid_bias"][:], ps[:, 3, 0:1], b1c[:], ALU.add), "hid_bias1", "ld_b1f")
    for a, n in ((0, 512), (512, 256)):
        for j in range(KT):
            pe(f"gh{a}_{j}", lambda e, a=a, n=n, j=j: e.matmul(
                ps[0:SLOTS, 4 + a // 512, 0:n], slotT[:, j, :], whh[:, j, a:a + n],
                start=(j == 0), stop=(j == KT - 1)), "slotT", "ld_whh")
    k["gate_bias"], k["half_hn"], k["new_bias"] = (sb("gate_bias", [SLOTS, 512]), sb("half_hn", [SLOTS, D]),
                                                   sb("new_bias", [SLOTS, D]))
    dve("gate_b1", lambda e: e.tensor_tensor(k["gate_bias"][:], ps[0:SLOTS, 4, :], bhh[:, 0:512], ALU.add),
        "gh0_1", "ld_bhh")
    dve("gate_b2", lambda e: e.tensor_tensor(k["gate_bias"][:], k["gate_bias"][:], bih[:, 0:512], ALU.add),
        "gate_b1", "ld_bih")
    dve("half_hn1", lambda e: e.tensor_tensor(k["half_hn"][:], ps[0:SLOTS, 5, 0:D], bhh[:, 512:768], ALU.add), "gh512_1")
    dve("half_hn2", lambda e: e.tensor_scalar(k["half_hn"][:], k["half_hn"][:], 0.5, None, ALU.mult), "half_hn1")
    dve("new_bias", lambda e: e.tensor_copy(k["new_bias"][:], bih[:, 512:768]), "ld_bih")

    wv, wo, bv, bvw = tmp("wvf", [128, KT, D]), tmp("wofT", [128, KT, D]), tmp("bvf_c", [128, KT]), tmp("bvf_w", [128, KT, SLOTS])
    load("ld_wvf", wv[:], tiles(inp["wvf"]))
    load("ld_wofT", wo[:], tiles(inp["wofT"]))
    load("ld_bvf", bv[:], inp["bvf"])
    k["wvo"], k["bvo"] = sb("wvo", [128, KT, D]), sb("bvo", [SLOTS, D])
    for i in range(KT):
        for j in range(KT):
            pe(f"wvo{i}{j}", lambda e, i=i, j=j: e.matmul(ps[:, 6, D * i:D * i + D], wv[:, j, 128 * i:128 * i + 128],
                                                          wo[:, j, :], start=(j == 0), stop=(j == KT - 1)),
               "ld_wvf", "ld_wofT")
    dve("wvo", lambda e: e.tensor_copy(k["wvo"][:], ps[:, 6, :].rearrange("p (k n) -> p k n", k=KT)), "wvo11")
    for j in range(KT):
        dve(f"bvw{j}", lambda e, j=j: e.tensor_scalar(bvw[:, j, :], k["ones"][:, 0:SLOTS], bv[:, j:j + 1], None, ALU.mult),
            "ones", "ld_bvf")
    for j in range(KT):
        pe(f"bvo{j}", lambda e, j=j: e.matmul(ps[0:SLOTS, 7, 0:D], bvw[:, j, :], wo[:, j, :],
                                              start=(j == 0), stop=(j == KT - 1)), "bvw1")
    dve("bvo", lambda e: e.tensor_copy(k["bvo"][:], ps[0:SLOTS, 7, 0:D]), "bvo1")
    tau = tmp("tau_c", [128, 1])
    k["inv_tau"] = sb("inv_tau", [128, 1])
    load("ld_tau", tau[:], rows(inp["tau"]))
    act("tau1", lambda e: e.activation(tau[:], tau[:], ACT.Abs), "ld_tau")
    dve("tau2", lambda e: e.tensor_scalar(tau[:], tau[:], 0.1, None, ALU.add), "tau1")
    dve("inv_tau", lambda e: e.reciprocal(k["inv_tau"][:], tau[:]), "tau2")

    for name, n, shape in (("w1t", HID * KT, [128, KT, HID]), ("w2t", HT * D, [128, HT, D])):
        w, a = tmp("f_" + name, [128, n]), tmp("a_" + name, [128, 1])
        k[name] = sb(name, [128, n], BF16)
        k[name + "_mean"] = sb(name + "_mean", [128, 1])
        bank = 6 if name == "w1t" else 7
        load("ld_" + name, w[:].rearrange("p (k n) -> p k n", k=shape[1]), tiles(inp[name]))
        dve(name + "1", lambda e, w=w, a=a: e.tensor_reduce(a[:], w[:], AX.X, ALU.add, apply_absolute_value=True), "ld_" + name)
        pe(name + "2", lambda e, a=a, bank=bank: e.matmul(ps[:, bank, 0:1], k["ones"][:], a[:], start=True, stop=True),
           name + "1", "wvo", "bvo")
        dve(name + "3", lambda e, name=name, bank=bank: e.tensor_scalar(
            k[name + "_mean"][:], ps[:, bank, 0:1], 1.0 / (HID * D), 1e-5, ALU.mult, ALU.max), name + "2")
        dve(name + "4", lambda e, name=name, a=a: e.reciprocal(a[:], k[name + "_mean"][:]), name + "3")
        dve(name + "5", lambda e, w=w, a=a: e.tensor_scalar(w[:], w[:], a[:, 0:1], ROUND, ALU.mult, ALU.add), name + "4")
        dve(name + "6", lambda e, w=w: e.tensor_scalar(w[:], w[:], -ROUND, 1.0, ALU.add, ALU.min), name + "5")
        dve(name + "7", lambda e, w=w, name=name: e.tensor_scalar(k[name][:], w[:], -1.0, None, ALU.max), name + "6")
    for name, f in (("w1t", 1.0 / 127), ("w2t", 0.5 / 127)):
        k[name + "_back"] = sb(name + "_back", [128, 1])
        dve(name + "_back", lambda e, name=name, f=f: e.tensor_scalar(
            k[name + "_back"][:], k[name + "_mean"][:], f, None, ALU.mult), name + "3")
    for name in ("conv_w", "conv_b"):
        k[name] = sb(name, [128, HT, 3] if name == "conv_w" else [128, HT])
        load("ld_" + name, k[name][:], inp[name])


def buffers(sb, label):
    t = {}
    for name, shape, dt in (
        ("x_in", [128, D], F32), ("ctx", [128, D], F32), ("mask_r", [128, T], F32), ("mask_c", [128, 1], F32),
        ("mask_bf", [128, T], BF16), ("xb", [128, D], F32), ("xa", [128, D], F32), ("xn", [128, D], F32),
        ("xnT", [128, KT, T], F32), ("ctxT", [128, KT, T], F32), ("stat", [128, 6], F32), ("sv", [128, 4], F32),
        ("qT", [128, KT, T], F32), ("kp", [128, KT, T + 2 * PAD], F32), ("vp", [128, KT, T + 2 * PAD], F32),
        ("va", [128, H, VC], F32), ("neg_min", [128, GROUPS, PER], F32), ("sums", [128, H], F32), ("fw3", [128, 4, 96], BF16),
        ("o", [128, D], F32), ("oT", [128, KT, T], F32), ("out", [128, D], F32), ("qs", [128, 8], F32),
    ):
        t[name] = sb(f"{label}_{name}", shape, dt)
    stages = (
        (("prod", [128, WIN, KT, T], F32), ("wsc", [128, WIN, H], F32), ("wsm", [128, 5, H], F32), ("wre", [128, WIN, H], F32),
         ("fwT", [96, 4, T], BF16), ("scT", [128, 4, T], F32)),
        (("p", [128, 2, PER, T], F32), ("pT", [128, PER, T], F32), ("s", [128, PER * T], F32), ("kx", [128, KT, 2, T], F32),
         ("oU", [128, GROUPS, T], F32)),
        (("lg", [128, 3, SLOTS], F32), ("top", [128, 8], F32), ("sc1", [128, 4], F32), ("hT", [128, T], F32),
         ("al", [128, SLOTS], F32), ("alT", [SLOTS, T], F32), ("giT", [128, KT, SLOTS], F32), ("rws", [SLOTS, 2], F32),
         ("rz", [SLOTS, 512], F32), ("nw", [SLOTS, 3, D], F32), ("hnT", [128, KT, SLOTS], F32), ("sval", [SLOTS, D], F32)),
        (("hp", [128, HT, T + 2], F32), ("cv", [128, HT, T], F32), ("hid", [128, HT, T], F32), ("xqb", [128, D], BF16),
         ("xqT", [128, KT, T], BF16), ("dg", [128, T], F32), ("back", [128, T], F32)),
        (("hqb", [128, HID], BF16), ("hqT", [128, HT, T], BF16), ("gap", [128, 2 * HT], F32), ("xq", [128, D], F32)),
    )

    def words(shape, dt):
        n = int(np.prod(shape[1:]))
        return n if dt == F32 else n // 2

    size = max(sum(words(shape, dt) for _, shape, dt in stage) for stage in stages)
    arena = sb(f"{label}_arena", [128, size])
    for stage in stages:
        at = 0
        for name, shape, dt in stage:
            n = words(shape, dt)
            v = arena[0:shape[0], at:at + n]
            if dt != F32:
                v = v.bitcast(dt)
            if len(shape) == 3:
                v = v.rearrange("p (a b) -> p a b", a=shape[1])
            elif len(shape) == 4:
                v = v.rearrange("p (a b c) -> p a b c", a=shape[1], b=shape[2])
            t[name] = v
            at += n
    return t


def sequence_steps(ch, t, ps, k, dram):

    def dve(name, emit, *after, n=256, plain=False):
        return ch.step(DVE, name, lambda e, _: emit(e), after, cost=0.07 + n / 960, plain=plain)

    def act(name, emit, *after, n=256):
        return ch.step(ACTE, name, lambda e, _: emit(e), after, cost=0.05 + n / 1200)

    def pool(name, emit, *after, n=256, plain=False):
        return ch.step(POOL, name, lambda e, _: emit(e), after, cost=0.1 + n / 450, plain=plain)

    def mm(name, out, lhsT, rhs, *after, start=True, stop=True, passes=4, cost=None):
        n = max(lhsT.free_size() if passes == 4 else 1, rhs.free_size())
        return ch.step(PE, name, lambda e, _: e.matmul(out, lhsT, rhs, start=start, stop=stop),
                       after, cost=cost or passes * n / 2400)

    def flip(name, out, src, *after, ident=None):
        rows = src.shape[0]
        ident = (k["ident"] if ident is None else ident)[0:rows, 0:rows]
        return ch.step(PE, name, lambda e, _: e.transpose(out, src, ident), after, cost=0.107 if src.dtype == F32 and rows == 128 else 0.053, plain=rows < 128)

    def meanwhile(name, bank, *after):
        ch.meanwhile(name, lambda e, _: e.matmul(ps[:, bank, :], k["ones_bf"][0:96, :], k["expand_bf"][:].rearrange("p a b -> p (a b)"),
                                                 start=True, stop=True), after)

    def layer_norm(tag, x, ready, bank_free):
        dve(tag + "_st", lambda e: e.bn_stats(t["stat"][:, 0:6], x), *ready)
        dve(tag + "_mv", lambda e: e.bn_aggr(t["sv"][:, 0:2], t["stat"][:, 0:6]), tag + "_st", n=8, plain=True)
        dve(tag + "_ve", lambda e: e.tensor_scalar(t["sv"][:, 2:3], t["sv"][:, 1:2], LN_EPS, None, ALU.add), tag + "_mv", n=8)
        ch.step(POOL, tag + "_rs", lambda e, _: e.tensor_tensor(t["sv"][:, 3:4], t["sv"][:, 2:3], k["neg_half"][:], ALU.pow),
                [tag + "_ve"], cost=0.46)
        dve(tag + "_xn", lambda e: e.tensor_scalar(t["xn"][:], x, t["sv"][:, 0:1], t["sv"][:, 3:4],
                                                   ALU.subtract, ALU.mult), tag + "_rs")
        for j in range(KT):
            flip(f"{tag}_T{j}", ps[:, 1, T * j:T * j + T], t["xn"][:, 128 * j:128 * j + 128], tag + "_xn", *bank_free)

    def copy_xnT(tag):
        act(tag + "_xnT", lambda e: e.copy(t["xnT"][:], ps[:, 1, 0:D].rearrange("p (k t) -> p k t", k=KT)), f"{tag}_T1")

    def residual_in(tag, x, bias, ready):
        pool(tag + "_xb", lambda e: e.tensor_tensor(t["xb"][:], x, bias[:], ALU.add), *ready)

    def project(tag, w, lhsT, bank, ready):
        for j in range(KT):
            mm(f"{tag}_pr{j}", ps[:, bank, 0:D], lhsT[:, j, :], w[:, j, :], *ready, start=(j == 0), stop=(j == KT - 1))

    def attention(tag, ready, bias=None, masked=False, scale_rows=False):

        def scores(g):
            r = 32 * g
            free = [f"{tag}_ex{g - 1}_{PER - 1}" if bias is None else f"{tag}_bi{g - 1}"] if g else []
            for j in range(KT):
                out = ps[:, 0, D * j:D * j + D]
                if masked:
                    mm(f"{tag}_mk{g}{j}", out, k["ones_bf"][r:r + 1, :], spread(t["mask_bf"][r:r + 1, :], 1, 2),
                       "mask_bf", *ready, *free, stop=False, passes=1)
                if j == 0 and g:
                    meanwhile(f"{tag}_{'mk' if masked else 's'}{g}0", 1, *([f"{tag}_ou{g - 2}"] if g >= 2 else ready))
                mm(f"{tag}_s{g}{j}", out, t["qT"][r:r + 32, j, :], t["kx"][r:r + 32, j, :, :].rearrange("p o t -> p (o t)"),
                   *ready, *free, start=not masked)
            src = ps[:, 0, :]
            last = f"{tag}_s{g}1"
            if bias is not None:
                dve(f"{tag}_bi{g}", lambda e: e.tensor_tensor(
                    t["s"][:], ps[:, 0, :], bias[:, g, :, :, :].rearrange("p j o t -> p (j o t)"), ALU.add),
                    last, *([f"{tag}_ex{g - 1}_{PER - 1}"] if g else []), n=512)
                src, last = t["s"][:], f"{tag}_bi{g}"
            src = src.rearrange("p (a t) -> p a t", t=T)
            dve(f"{tag}_mx{g}", lambda e: e.tensor_reduce(t["neg_min"][:, g, :], src, AX.X, ALU.min), last, n=512)
            for a in range(PER):
                act(f"{tag}_ex{g}_{a}", lambda e, a=a: e.activation(
                    t["p"][:, g % 2, a, :], src[:, a, :], ACT.Exp, scale=-1.0, bias=t["neg_min"][:, g, a:a + 1]),
                    f"{tag}_mx{g}", *([f"{tag}_pT{g - 2}_{PER - 1}"] if g >= 2 else []), n=T + 112)

        def turn(g):
            meanwhile(f"{tag}_pT{g}_0", 1, *([f"{tag}_ou{g - 1}"] if g else ready))
            for a in range(PER):
                flip(f"{tag}_pT{g}_{a}", ps[:, 1, T * a:T * a + T], t["p"][:, g % 2, a, :], f"{tag}_ex{g}_{a}",
                     *([f"{tag}_ou{g - 1}"] if g else []))
            act(f"{tag}_pc{g}", lambda e: e.copy(t["pT"][:].rearrange("p a t -> p (a t)"), ps[:, 1, :]),
                f"{tag}_pT{g}_{PER - 1}", *([f"{tag}_pv{g - 1}_{PER - 1}"] if g else []), n=512)

        def values(g):
            for a in range(PER):
                h = 8 * (a // 2) + 2 * g + a % 2
                mm(f"{tag}_pv{g}_{a}", ps[VC * a:VC * a + VC, 1, 0:T], t["va"][:, h, :], t["pT"][:, a, :], f"{tag}_pc{g}", *ready,
                   cost=0.05 if a else None)
            act(f"{tag}_ou{g}", lambda e: e.copy(t["oU"][:, g, :], ps[:, 1, 0:T]), f"{tag}_pv{g}_{PER - 1}", n=128)

        scores(0)
        for g in range(GROUPS):
            if g + 1 < GROUPS:
                scores(g + 1)
            turn(g)
            values(g)
        for g in range(GROUPS):
            flip(f"{tag}_uT{g}", ps[:, 0, T * g:T * g + T], t["oU"][:, g, :], f"{tag}_ou{g}", f"{tag}_ex{GROUPS - 1}_{PER - 1}")
        meanwhile(f"{tag}_uT0", 0, f"{tag}_ex{GROUPS - 1}_{PER - 1}")
        meanwhile(f"{tag}_oT0", 1, f"{tag}_ou{GROUPS - 1}")
        meanwhile(f"{tag}_pr0", 0, f"{tag}_o1")
        u = ps[:, 0, :].rearrange("p (g j o c) -> p g j o c", g=GROUPS, j=KT, o=2)
        sums = t["sums"][:].rearrange("p (g j o) -> p g j o", g=GROUPS, j=KT)
        dve(tag + "_rc", lambda e: e.reciprocal(sums, u[:, :, :, :, DH]), f"{tag}_uT{GROUPS - 1}", n=16)
        norm = tag + "_rc"
        if scale_rows:
            dve(tag + "_rm", lambda e: e.tensor_scalar(t["sums"][:], t["sums"][:], t["mask_c"][:, 0:1], None, ALU.mult),
                norm, "mask_c", n=16)
            norm = tag + "_rm"
        o = t["o"][:].rearrange("p (j g o c) -> p g j o c", j=KT, g=GROUPS, o=2)
        for j in range(KT):
            dve(f"{tag}_o{j}", lambda e, j=j: e.tensor_tensor(o[:, :, j], u[:, :, j, :, 0:DH], spread(sums[:, :, j, :], 3, DH),
                                                              ALU.mult), norm, n=128)
            flip(f"{tag}_oT{j}", ps[:, 1, T * j:T * j + T], t["o"][:, 128 * j:128 * j + 128], f"{tag}_o{j}")
        act(tag + "_oc", lambda e: e.copy(t["oT"][:], ps[:, 1, 0:D].rearrange("p (k t) -> p k t", k=KT)), f"{tag}_oT1")

    def keys(tag, src, ready, bias=None):
        for o in range(2):
            if bias is None:
                act(f"{tag}_kx{o}", lambda e, o=o: e.activation(t["kx"][:, :, o, :], src, ACT.Copy,
                                                               scale=k["parity"][:, o:o + 1]), *ready, n=420)
                continue
            for j in range(KT):
                act(f"{tag}_kx{o}{j}", lambda e, o=o, j=j: e.activation(
                    t["kx"][:, j, o, :], src[:, j, :], ACT.Identity, scale=k["parity"][:, o:o + 1],
                    bias=bias[:, j, o:o + 1]), *ready, n=350)

    first = ("before", "y")

    layer_norm("a", t["x_in"][:], ["x_in", first], [first])
    copy_xnT("a")
    residual_in("a", t["x_in"][:], k["bo0_r"], ["x_in", first])
    for i, part in enumerate("qkv"):
        for m in range(KT):
            for j in range(KT):
                c0 = D * i + 128 * m
                out = ps[:, 0 if i < 2 else 1, D * (i % 2) + T * m:D * (i % 2) + T * m + T]
                mm(f"a_{part}{m}{j}", out, k["wqkv0T"][:, j, c0:c0 + 128], t["xnT"][:, j, :], "a_xnT",
                   start=(j == 0), stop=(j == KT - 1))
    act("a_qT", lambda e: e.copy(t["qT"][:], ps[:, 0, 0:D].rearrange("p (k t) -> p k t", k=KT)), "a_k11")
    act("a_kp", lambda e: e.copy(t["kp"][:, :, PAD:PAD + T], ps[:, 0, D:2 * D].rearrange("p (k t) -> p k t", k=KT)), "a_k11")
    act("a_vp", lambda e: e.copy(t["vp"][:, :, PAD:PAD + T], ps[:, 1, 0:D].rearrange("p (k t) -> p k t", k=KT)), "a_v11")
    WD = 5
    dve("a_qk", lambda e: e.tensor_tensor(t["prod"][:, 0:WD], spread(t["qT"][:], 1, WD), windows(t["kp"], 0, WD), ALU.mult),
        "a_qT", "a_kp", n=256 * WD)
    pool("a_qk2", lambda e: e.tensor_tensor(t["prod"][:, WD:WIN], spread(t["qT"][:], 1, WIN - WD),
                                            windows(t["kp"], WD, WIN - WD), ALU.mult), "a_qT", "a_kp", n=256 * (WIN - WD))
    for b, (w0, n) in enumerate(((0, 4), (4, 3))):
        for j in range(KT):
            r = 32 * (KT * b + j)
            mm(f"a_sc{b}{j}", ps[r:r + 32, 0, 0:T * n], k["head_sum"][:, 32 * j:32 * j + 32], t["prod"][:, w0:w0 + n, j, :],
               "a_qk", "a_qk2", "a_kp", cost=None if b == j == 0 else 0.05)
    act("a_s0", lambda e: e.copy(t["scT"][:, 0:3, :], ps[:, 0, 0:3 * T].rearrange("p (w t) -> p w t", t=T)), "a_sc11", n=384)
    act("a_s1", lambda e: e.copy(t["scT"][0:64, 3, :], ps[0:64, 0, 3 * T:]), "a_sc11", n=128)
    for w in range(3):
        flip(f"a_st{w}", ps[:, 1, T * w:T * w + T], t["scT"][:, w, :], "a_s0", "a_vp")
    flip("a_st3", ps[:, 1, 3 * T:3 * T + 64], t["scT"][0:64, 3, :], "a_s1")
    sm, ws, raw = t["wsm"], t["wsc"], t["wre"]
    sc = ps[:, 1, :].rearrange("p (w b j h) -> p w b j h", w=4, b=2, j=KT)
    for b, (w0, n) in enumerate(((0, 4), (4, 3))):
        dve(f"a_cp{b}", lambda e, b=b, w0=w0, n=n: e.tensor_copy(
            raw[:, w0:w0 + n, :].rearrange("p w (j h) -> p w j h", j=KT), sc[:, 0:n, b, :, 0:8]), "a_st3", n=64)
    by_head = ws[:].rearrange("p w h -> p h w")
    dve("a_mx", lambda e: e.tensor_reduce(sm[:, 0, :], raw[:].rearrange("p w h -> p h w"), AX.X, ALU.max), "a_cp1", n=112)
    dve("a_sub", lambda e: e.tensor_tensor(ws[:], raw[:], spread(sm[:, 0, :], 1, WIN), ALU.subtract), "a_mx", n=112)
    act("a_exp", lambda e: e.activation(ws[:], ws[:], ACT.Exp, scale=0.25), "a_sub", n=112)
    dve("a_sum", lambda e: e.tensor_reduce(sm[:, 1, :], by_head, AX.X, ALU.add), "a_exp", n=112)
    dve("a_cn", lambda e: e.tensor_tensor(ws[:], ws[:], k["conn"][:].rearrange("p (w h) -> p w h", h=H), ALU.mult),
        "a_exp", "a_sum", n=112)
    dve("a_sumc", lambda e: e.tensor_reduce(sm[:, 2, :], by_head, AX.X, ALU.add), "a_cn", n=112)
    dve("a_den", lambda e: e.scalar_tensor_tensor(out=sm[:, 3, :], in0=sm[:, 1, :], scalar=1e-9, in1=sm[:, 2, :],
                                                  op0=ALU.mult, op1=ALU.add), "a_sumc", n=16)
    dve("a_rec", lambda e: e.reciprocal(sm[:, 4, :], sm[:, 3, :]), "a_den", n=16)
    dve("a_fw", lambda e: e.tensor_tensor(ws[:], ws[:], spread(sm[:, 4, :], 1, WIN), ALU.mult), "a_rec", n=112)
    f3 = t["fw3"][:].rearrange("p i c -> p (i c)")[:, 0:WIN * KT * 24].rearrange("p (w j s h) -> p w j s h", w=WIN, j=KT, s=3)
    w4, re = ws[:].rearrange("p w (j h) -> p w j h", j=KT), t["wre"][:].rearrange("p w (j h) -> p w j h", j=KT)
    dve("a_f1", lambda e: e.tensor_copy(f3[:, :, :, 0, :], w4), "a_fw", n=112)
    dve("a_r1", lambda e: e.tensor_tensor(re, w4, f3[:, :, :, 0, :], ALU.subtract), "a_f1", n=112)
    dve("a_f2", lambda e: e.tensor_copy(f3[:, :, :, 1, :], re), "a_r1", n=112)
    dve("a_f3", lambda e: e.tensor_tensor(f3[:, :, :, 2, :], re, f3[:, :, :, 1, :], ALU.subtract), "a_f2", n=112)
    half1 = ps[:, 1, :].bitcast(BF16)
    for i in range(4):
        flip(f"a_fT{i}", half1[0:96, T * i:T * i + T], t["fw3"][:, i, :], "a_f3", ident=k["ident_bf"])
    act("a_fc", lambda e: e.copy(t["fwT"][:], half1[0:96, 0:4 * T].rearrange("p (i t) -> p i t", i=4)), "a_fT3", n=512)
    for q in range(4):
        n = min(2, WIN - 2 * q)
        for w in range(2 * q, 2 * q + n):
            for j in range(KT):
                c0 = D * (w % 2) + T * j
                mm(f"a_e{w}{j}", ps[:, q % 2, c0:c0 + T], k["expand_bf"][:, (w * KT + j) % 4, :],
                   t["fwT"][:, (w * KT + j) // 4, :], "a_fc", "a_vp", f"a_pv{q - 2}" if q >= 2 else "a_s1", passes=1)
        dve(f"a_pv{q}", lambda e, q=q, n=n: e.tensor_tensor(
            t["prod"][:, 2 * q:2 * q + n], ps[:, q % 2, 0:D * n].rearrange("p (w j t) -> p w j t", w=n, j=KT),
            windows(t["vp"], 2 * q, n), ALU.mult), f"a_e{2 * q + n - 1}1", n=256 * n)
    dve("a_o3", lambda e: e.tensor_tensor(t["prod"][:, 0:3], t["prod"][:, 0:3], t["prod"][:, 3:6], ALU.add), "a_pv2", n=768)
    pool("a_o1", lambda e: e.tensor_tensor(t["prod"][:, 6], t["prod"][:, 6], t["prod"][:, 0], ALU.add), "a_pv3", "a_o3")
    dve("a_o2", lambda e: e.tensor_tensor(t["prod"][:, 1], t["prod"][:, 1], t["prod"][:, 2], ALU.add), "a_o3")
    dve("a_oT", lambda e: e.tensor_tensor(t["oT"][:], t["prod"][:, 1], t["prod"][:, 6], ALU.add), "a_o2", "a_o1")
    project("a", k["wo0T"], t["oT"], 0, ["a_oT"])
    dve("a_y", lambda e: e.tensor_tensor(t["xa"][:], ps[:, 0, 0:D], t["xb"][:], ALU.add), "a_pr1", "a_xb")

    layer_norm("b", t["xa"][:], ["a_y"], ["a_pv3"])
    act("b_q", lambda e: e.activation(t["qT"][:], ps[:, 1, 0:D].rearrange("p (k t) -> p k t", k=KT), ACT.Copy, scale=-0.25),
        "b_T1")
    for j in range(KT):
        flip(f"c_T{j}", ps[:, 0, T * j:T * j + T], t["ctx"][:, 128 * j:128 * j + 128], "ctx", "a_y")
    act("c_T", lambda e: e.copy(t["ctxT"][:], ps[:, 0, 0:D].rearrange("p (k t) -> p k t", k=KT)), "c_T1")
    keys("b", t["ctxT"][:], ["c_T"])
    dve("mask_bf", lambda e: e.tensor_scalar(t["mask_bf"][:], t["mask_r"][:], 0.0, MASKED, ALU.is_equal, ALU.mult),
        "mask_r", first, n=128)
    va_cols = t["va"][:, :, 0:DH]
    dve("b_va", lambda e: e.tensor_scalar(va_cols, t["ctx"][:].rearrange("p (h c) -> p h c", c=DH), t["mask_c"][:, 0:1], None,
                                          ALU.mult), "ctx", "mask_c", first)
    pool("b_xb1", lambda e: e.tensor_scalar(t["out"][:], k["bp_r"][:], t["mask_c"][:, 0:1], 0.0, ALU.mult, ALU.add),
         "mask_c", ("before", "store"), plain=True)
    pool("b_xb", lambda e: e.tensor_tensor(t["xb"][:], t["xa"][:], t["out"][:], ALU.add), "b_xb1", "a_y")
    attention("b", ["b_q", "b_kx1", "b_va"], masked=True, scale_rows=True)
    project("b", k["wpT"], t["oT"], 0, ["b_oc"])
    dve("b_y", lambda e: e.scalar_tensor_tensor(out=t["xa"][:], in0=ps[:, 0, 0:D], scalar=t["mask_c"][:, 0:1],
                                                in1=t["xb"][:], op0=ALU.mult, op1=ALU.add), "b_pr1", "b_xb")

    layer_norm("f", t["xa"][:], ["b_y"], ["b_y"])
    copy_xnT("f")
    residual_in("f", t["xa"][:], k["bof_r"], ["b_y"])
    for j in range(KT):
        mm(f"f_h{j}", ps[:, 0, 0:T], k["w1aT"][:, j, :], t["xnT"][:, j, :], "f_xnT", start=(j == 0), stop=(j == KT - 1))
    act("f_gelu", lambda e: e.activation(t["hT"][:], ps[:, 0, 0:T], ACT.Gelu, bias=k["hid_bias"][:, 0:1]), "f_h1", n=1750)
    mm("f_lg", ps[:, 1, 0:SLOTS], t["hT"][:], k["w2fT"][:], "f_gelu")
    lg = t["lg"]
    dve("f_l", lambda e: e.tensor_tensor(lg[:, 0, :], ps[:, 1, 0:SLOTS], k["b2f_r"][:], ALU.add), "f_lg", n=64)
    dve("f_top", lambda e: e.max(t["top"][:], lg[:, 0, :]), "f_l", n=64, plain=True)
    dve("f_mr", lambda e: e.match_replace(lg[:, 1, :], t["top"][:], lg[:, 0, :], -3e38), "f_top", n=128, plain=True)
    dve("f_nm", lambda e: e.tensor_scalar(t["sc1"][:, 0:1], t["top"][:, 0:1], k["inv_tau"][:, 0:1], -1.0, ALU.mult, ALU.mult),
        "f_top", n=8)
    act("f_e", lambda e: e.activation(lg[:, 2, :], lg[:, 0, :], ACT.Exp, scale=k["inv_tau"][:, 0:1], bias=t["sc1"][:, 0:1]),
        "f_nm", n=200)
    dve("f_m", lambda e: e.tensor_tensor(lg[:, 1, :], lg[:, 1, :], lg[:, 0, :], ALU.is_lt), "f_mr", n=64)
    dve("f_em", lambda e: e.tensor_tensor(lg[:, 2, :], lg[:, 2, :], lg[:, 1, :], ALU.mult), "f_m", "f_e", n=64)
    dve("f_s", lambda e: e.tensor_reduce(t["sc1"][:, 1:2], lg[:, 2, :], AX.X, ALU.add), "f_em", n=64)
    dve("f_r", lambda e: e.reciprocal(t["sc1"][:, 2:3], t["sc1"][:, 1:2]), "f_s", n=8)
    dve("f_al", lambda e: e.tensor_scalar(t["al"][:], lg[:, 2, :], t["sc1"][:, 2:3], None, ALU.mult), "f_r", n=64)
    for j in range(KT):
        mm(f"f_gi{j}", ps[:, 0, SLOTS * j:SLOTS * j + SLOTS], t["xn"][:, 128 * j:128 * j + 128], t["al"][:], "f_al")
    mm("f_ws", ps[0:SLOTS, 1, 64:65], t["al"][:], k["ones"][:, 0:1], "f_al")
    flip("f_alT", ps[0:SLOTS, 1, T:2 * T], t["al"][:], "f_al")
    act("f_giT", lambda e: e.copy(t["giT"][:], ps[:, 0, 0:KT * SLOTS].rearrange("p (k s) -> p k s", k=KT)), "f_gi1", n=128)
    dve("f_w1", lambda e: e.tensor_scalar(t["rws"][:, 0:1], ps[0:SLOTS, 1, 64:65], 1e-8, None, ALU.add), "f_alT", n=8)
    dve("f_w2", lambda e: e.reciprocal(t["rws"][:, 1:2], t["rws"][:, 0:1]), "f_w1", n=8)
    dve("f_ac", lambda e: e.tensor_copy(t["alT"][:], ps[0:SLOTS, 1, T:2 * T]), "f_alT", n=128)
    for a, n, bank in ((0, 512, 0), (512, 256, 1)):
        for j in range(KT):
            mm(f"f_gx{a}_{j}", ps[0:SLOTS, bank, 0:n], t["giT"][:, j, :], k["wihT"][:, j, a:a + n], "f_giT", "f_ac",
               start=(j == 0), stop=(j == KT - 1))
    dve("f_rz1", lambda e: e.scalar_tensor_tensor(out=t["rz"][:], in0=ps[0:SLOTS, 0, :], scalar=t["rws"][:, 1:2],
                                                  in1=k["gate_bias"][:], op0=ALU.mult, op1=ALU.add), "f_gx0_1", "f_w2", n=512)
    act("f_rz", lambda e: e.activation(t["rz"][:], t["rz"][:], ACT.Tanh, scale=0.5), "f_rz1", n=512)
    nw, tr, tz = t["nw"], t["rz"][:, 0:D], t["rz"][:, D:2 * D]
    dve("f_n1", lambda e: e.scalar_tensor_tensor(out=nw[:, 0, :], in0=ps[0:SLOTS, 1, 0:D], scalar=t["rws"][:, 1:2],
                                                 in1=k["new_bias"][:], op0=ALU.mult, op1=ALU.add), "f_gx512_1")
    dve("f_n2", lambda e: e.scalar_tensor_tensor(out=nw[:, 1, :], in0=tr, scalar=1.0, in1=k["half_hn"][:],
                                                 op0=ALU.add, op1=ALU.mult), "f_rz")
    dve("f_n3", lambda e: e.tensor_tensor(nw[:, 1, :], nw[:, 1, :], nw[:, 0, :], ALU.add), "f_n2", "f_n1")
    act("f_n", lambda e: e.activation(nw[:, 0, :], nw[:, 1, :], ACT.Tanh), "f_n3")
    dve("f_u1", lambda e: e.tensor_tensor(nw[:, 1, :], k["slots"][:], nw[:, 0, :], ALU.subtract), "f_n")
    dve("f_u2", lambda e: e.scalar_tensor_tensor(out=nw[:, 2, :], in0=tz, scalar=1.0, in1=nw[:, 1, :],
                                                 op0=ALU.add, op1=ALU.mult), "f_u1")
    dve("f_u3", lambda e: e.scalar_tensor_tensor(out=nw[:, 1, :], in0=nw[:, 2, :], scalar=0.5, in1=nw[:, 0, :],
                                                 op0=ALU.mult, op1=ALU.add), "f_u2")
    for j in range(KT):
        flip(f"f_hT{j}", ps[:, 0, SLOTS * j:SLOTS * j + SLOTS], nw[:, 1, 128 * j:128 * j + 128], "f_u3", "f_ac")
    act("f_hc", lambda e: e.copy(t["hnT"][:], ps[:, 0, 0:KT * SLOTS].rearrange("p (k s) -> p k s", k=KT)), "f_hT1", n=128)
    for j in range(KT):
        mm(f"f_sv{j}", ps[0:SLOTS, 1, 0:D], t["hnT"][:, j, :], k["wvo"][:, j, :], "f_hc", "f_w1",
           start=(j == 0), stop=(j == KT - 1))
    dve("f_sv", lambda e: e.tensor_tensor(t["sval"][:], ps[0:SLOTS, 1, 0:D], k["bvo"][:], ALU.add), "f_sv1")
    mm("f_o", ps[:, 0, 0:D], t["alT"][:], t["sval"][:], "f_sv", "f_ac", "f_hc")
    dve("f_y", lambda e: e.tensor_tensor(t["xa"][:], ps[:, 0, 0:D], t["xb"][:], ALU.add), "f_o", "f_xb")

    def dense_qkv(tag, w, kv, ready, bias_v):
        for i, src in ((0, t["xnT"]), (1, kv)):
            for m in range(KT):
                for j in range(KT):
                    mm(f"{tag}_{'qk'[i]}{m}{j}", ps[:, 0, D * i + T * m:D * i + T * m + T], w[:, j, D * i + 128 * m:D * i + 128 * m + 128],
                       src[:, j, :], *ready, start=(j == 0), stop=(j == KT - 1))
        for j in range(KT):
            mm(f"{tag}_v{j}", ps[:, 1, 0:D], kv[:, j, :], w[:, j, 2 * D:3 * D], *ready, start=(j == 0), stop=(j == KT - 1))
        for m in range(KT):
            act(f"{tag}_qc{m}", lambda e, m=m: e.activation(
                t["qT"][:, m, :], ps[:, 0, T * m:T * m + T], ACT.Identity, scale=-0.25, bias=k["bq" + tag][:, m:m + 1]),
                f"{tag}_k11", n=200)
        keys(tag, ps[:, 0, D:2 * D].rearrange("p (k t) -> p k t", k=KT), [f"{tag}_k11"], bias=k["bk" + tag])
        dve(tag + "_va", lambda e: e.tensor_tensor(va_cols, ps[:, 1, 0:D].rearrange("p (h c) -> p h c", c=DH),
                                                   bias_v[:].rearrange("p (h c) -> p h c", c=DH), ALU.add), f"{tag}_v1")

    layer_norm("n", t["xa"][:], ["f_y"], ["f_y"])
    copy_xnT("n")
    residual_in("n", t["xa"][:], k["bproj_r"], ["f_y"])
    dense_qkv("1", k["wqkv1"], t["xnT"], ["n_xnT"], k["bv1_r"])
    attention("1", ["1_qc1", "1_kx11", "1_va"], bias=k["pos_bias"])
    project("1", k["wproj"], t["oT"], 0, ["1_oc"])
    dve("1_y", lambda e: e.tensor_tensor(t["xa"][:], ps[:, 0, 0:D], t["xb"][:], ALU.add), "1_pr1", "n_xb")

    layer_norm("m", t["xa"][:], ["1_y"], ["1_y"])
    copy_xnT("m")
    residual_in("m", t["xa"][:], k["box_r"], ["1_y"])
    dense_qkv("x", k["wqkvxT"], t["ctxT"], ["m_xnT"], k["bvx_r"])
    attention("x", ["x_qc1", "x_kx11", "x_va"])
    project("x", k["woxT"], t["oT"], 0, ["x_oc"])
    dve("x_y", lambda e: e.tensor_tensor(t["xa"][:], ps[:, 0, 0:D], t["xb"][:], ALU.add), "x_pr1", "m_xb")

    layer_norm_only = [("g_st", lambda e: e.bn_stats(t["stat"][:, 0:6], t["xa"][:]), ["x_y"], 256),
                       ("g_mv", lambda e: e.bn_aggr(t["sv"][:, 0:2], t["stat"][:, 0:6]), ["g_st"], 8),
                       ("g_ve", lambda e: e.tensor_scalar(t["sv"][:, 2:3], t["sv"][:, 1:2], LN_EPS, None, ALU.add), ["g_mv"], 8)]
    for name, emit, after, n in layer_norm_only:
        dve(name, emit, *after, n=n, plain=n == 8)
    ch.step(POOL, "g_rs", lambda e, _: e.tensor_tensor(t["sv"][:, 3:4], t["sv"][:, 2:3], k["neg_half"][:], ALU.pow),
            ["g_ve"], cost=0.46)
    dve("g_xn", lambda e: e.tensor_scalar(t["xn"][:], t["xa"][:], t["sv"][:, 0:1], t["sv"][:, 3:4], ALU.subtract, ALU.mult),
        "g_rs")
    qs = t["qs"]
    dve("g_am", lambda e: e.tensor_reduce(qs[:, 0:1], t["xn"][:], AX.X, ALU.max, apply_absolute_value=True), "g_xn")
    dve("g_cl", lambda e: e.tensor_scalar(qs[:, 0:1], qs[:, 0:1], 1e-5, None, ALU.max), "g_am", n=8)
    dve("g_rc", lambda e: e.reciprocal(qs[:, 1:2], qs[:, 0:1]), "g_cl", n=8)
    dve("g_sc", lambda e: e.tensor_scalar(qs[:, 2:3], qs[:, 1:2], 127.0, None, ALU.mult), "g_rc", n=8)
    dve("g_bk", lambda e: e.tensor_scalar(qs[:, 3:4], qs[:, 0:1], k["w1t_back"][:, 0:1], None, ALU.mult), "g_cl", n=8)
    dve("g_q1", lambda e: e.tensor_scalar(t["xq"][:], t["xn"][:], qs[:, 2:3], ROUND, ALU.mult, ALU.add), "g_sc")
    dve("g_q2", lambda e: e.tensor_scalar(t["xqb"][:], t["xq"][:], -ROUND, None, ALU.add), "g_q1")
    dve("g_dg", lambda e: e.tensor_scalar(t["dg"][:], k["ident"][:], qs[:, 3:4], None, ALU.mult), "g_bk", n=128)
    mm("g_bb", ps[:, 0, 0:T], k["ones"][:], t["dg"][:], "g_dg")
    act("g_bc", lambda e: e.copy(t["back"][:], ps[:, 0, 0:T]), "g_bb", n=128)
    half = ps[:, 1, :].bitcast(BF16)
    for j in range(KT):
        flip(f"g_T{j}", half[:, T * j:T * j + T], t["xqb"][:, 128 * j:128 * j + 128], "g_q2", ident=k["ident_bf"])
    act("g_xqT", lambda e: e.copy(t["xqT"][:], half[:, 0:D].rearrange("p (k t) -> p k t", k=KT)), "g_T1")
    for m in range(HT):
        for j in range(KT):
            mm(f"g_h{m}{j}", ps[:, m // 4, T * (m % 4):T * (m % 4) + T],
               k["w1t"][:, HID * j + 128 * m:HID * j + 128 * m + 128], t["xqT"][:, j, :], "g_xqT", "g_bc",
               start=(j == 0), stop=(j == KT - 1), passes=1)
    edge = bass.AP(t["hp"].tensor, t["hp"].offset, [list(t["hp"].ap[0]), [T + 2, HT], [T + 1, 2]])
    ch.step(POOL, "g_pad", lambda e, _: e.memset(edge, 0.0), ["g_xn"], cost=0.1, plain=True)
    cv, cwt = t["cv"], k["conv_w"]
    for q in range(2):
        m0 = 4 * q
        dve(f"g_hp{q}", lambda e, q=q, m0=m0: e.tensor_tensor(
            t["hp"][:, m0:m0 + 4, 1:1 + T], ps[:, q, :].rearrange("p (m t) -> p m t", t=T),
            spread(t["back"][:], 1, 4), ALU.mult), f"g_h{m0 + 3}1", "g_bc", n=512)
        for m in range(m0, m0 + 4):
            act(f"g_c{m}", lambda e, m=m: e.activation(cv[:, m, :], t["hp"][:, m, 1:1 + T], ACT.Identity,
                                                       scale=cwt[:, m, 1:2], bias=k["conv_b"][:, m:m + 1]), f"g_hp{q}", n=400)
        for tap, sh in ((0, 0), (2, 2)):
            for m in range(m0, m0 + 4):
                dve(f"g_t{tap}{m}", lambda e, m=m, tap=tap, sh=sh: e.scalar_tensor_tensor(
                    out=cv[:, m, :], in0=t["hp"][:, m, sh:sh + T], scalar=cwt[:, m, tap:tap + 1], in1=cv[:, m, :],
                    op0=ALU.mult, op1=ALU.add), f"g_c{m}" if tap == 0 else f"g_t0{m}", "g_pad", n=190)
    for q in range(2):
        v = slice(4 * q, 4 * q + 4)
        act(f"g_th{q}", lambda e, v=v: e.activation(t["hid"][:, v, :], cv[:, v, :], ACT.Tanh, scale=0.5), f"g_t2{4 * q + 3}", n=512)
        dve(f"g_si{q}", lambda e, v=v: e.scalar_tensor_tensor(
            out=t["hid"][:, v, :].rearrange("p m t -> p (m t)"), in0=t["hid"][:, v, :].rearrange("p m t -> p (m t)"), scalar=1.0,
            in1=cv[:, v, :].rearrange("p m t -> p (m t)"), op0=ALU.add, op1=ALU.mult), f"g_th{q}", n=512)
        for m in range(4 * q, 4 * q + 4):
            flip(f"g_hT{m}", ps[:, q, T * (m - 4 * q):T * (m - 4 * q) + T], t["hid"][:, m, :], f"g_si{q}")
    tok = ps[:, 0:2, :].rearrange("p a b -> p (a b)")
    dve("g_am2", lambda e: e.tensor_reduce(qs[:, 4:5], tok, AX.X, ALU.max, apply_absolute_value=True), "g_hT7", n=1024)
    dve("g_cl2", lambda e: e.tensor_scalar(qs[:, 4:5], qs[:, 4:5], 2e-5, None, ALU.max), "g_am2", n=8)
    dve("g_rc2", lambda e: e.reciprocal(qs[:, 5:6], qs[:, 4:5]), "g_cl2", n=8)
    dve("g_sc2", lambda e: e.tensor_scalar(qs[:, 6:7], qs[:, 5:6], 127.0, None, ALU.mult), "g_rc2", n=8)
    dve("g_bk2", lambda e: e.tensor_scalar(qs[:, 7:8], qs[:, 4:5], k["w2t_back"][:, 0:1], None, ALU.mult), "g_cl2", n=8)
    half0 = ps[:, 0, :].bitcast(BF16)
    flat = cv[:].rearrange("p m t -> p (m t)")
    dve("g_r1", lambda e: e.tensor_scalar(flat, tok, qs[:, 6:7], ROUND, ALU.mult, ALU.add), "g_sc2", "g_si1", n=1024)
    dve("g_r2", lambda e: e.tensor_scalar(t["hqb"][:], flat, -ROUND, None, ALU.add), "g_r1", n=512)
    for m in range(HT):
        flip(f"g_qT{m}", half0[:, T * m:T * m + T], t["hqb"][:, 128 * m:128 * m + 128], "g_r2", "g_xqT", ident=k["ident_bf"])
    act("g_qc", lambda e: e.copy(t["hqT"][:], half0[:, 0:HID].rearrange("p (m t) -> p m t", t=T)), "g_qT7", n=1024)
    for m in range(HT):
        mm(f"g_o{m}", ps[:, 1, 0:D], t["hqT"][:, m, :], k["w2t"][:, D * m:D * m + D], "g_qc", start=(m == 0), stop=(m == HT - 1),
           passes=1)
    dve("y", lambda e: e.scalar_tensor_tensor(out=t["out"][:], in0=ps[:, 1, 0:D], scalar=qs[:, 7:8], in1=t["xa"][:],
                                              op0=ALU.mult, op1=ALU.add), "g_o7", "g_bk2", "b_xb", ("before", "store"))
    for name, bank, after in (
        ("a_T0", 1, first), ("a_q00", 0, first), ("a_sc00", 0, "a_kp"), ("a_fT0", 0, "a_s1"), ("a_e00", 0, "a_s1"),
        ("a_pr0", 0, "a_pv2"), ("b_T0", 1, "a_pv3"), ("b_mk00", 0, "c_T"),
        ("f_T0", 1, "b_oc"), ("f_h0", 0, "b_y"), ("f_lg", 1, "f_xnT"), ("f_gi0", 0, "f_gelu"), ("f_hT0", 0, "f_rz1"),
        ("f_sv0", 1, "f_n1"), ("f_o", 0, "f_hc"), ("n_T0", 1, "f_sv"), ("1_q00", 0, "f_y"), ("m_T0", 1, "1_oc"),
        ("x_q00", 0, "1_y"), ("g_bb", 0, "x_y"), ("g_T0", 1, "x_oc"), ("g_h00", 0, "g_bc"), ("g_hT0", 0, "g_hp0"),
        ("g_hT4", 1, "g_hp1"), ("g_qT0", 1, "g_r1"), ("g_o0", 1, "g_r1"),
    ):
        meanwhile(name, bank, after)
    ch.step(ACTE, "store", lambda e, turn: e.dma_start(dram["out"](turn), t["out"][:]), ["y"], cost=0.1, count="store")


def decoder(nc, inp, x, ctx_in, mask, out):
    with ExitStack() as ctx:
        def opener(stack, side="left"):
            def sb(name, shape, dt=F32):
                return stack.enter_context(nc.sbuf_tensor(name, shape, dt, side=side))
            return sb

        nc.disable_value_cache = True
        sb = opener(ctx)
        ps = ctx.enter_context(nc.psum_tensor("banks", [128, 8, 512], F32))
        k = {}
        setup = Chain("setup")
        with ExitStack() as scratch:
            setup_steps(nc, setup, sb, opener(scratch, "right"), ps, inp, k)
        setup.open(nc, ctx)

        chains, tiles = [], []
        for c in range(NCHAIN):
            ch = Chain(f"chain{c}")
            t = buffers(sb, ch.label)
            by_turn = {name: ap.rearrange("(n c) t d -> n c t d", c=NCHAIN) for name, ap in
                       (("x", x), ("ctx", ctx_in), ("out", out))}
            mask_t = mask.rearrange("(n c) t -> n c t", c=NCHAIN)
            dram = {"out": lambda turn, c=c: by_turn["out"][turn, c]}
            ch.step(SP, "x_in", lambda e, turn, c=c, t=t: e.dma_start(t["x_in"][:], by_turn["x"][turn, c]),
                    [("before", "a_st"), ("before", "a_xn"), ("before", "a_xb")], count="x_in")
            ch.step(SP, "mask_r", lambda e, turn, c=c, t=t: e.dma_start(
                t["mask_r"][0:128:32, :], mask_t[turn, c].partition_broadcast(4)), [("before", "mask_bf")], count="mask_r")
            ch.step(SP, "mask_c", lambda e, turn, c=c, t=t: e.dma_start(
                t["mask_c"][:], mask_t[turn, c].rearrange("(t a) -> t a", a=1)), [("before", "b_y"), ("before", "b_xb1")], count="mask_c")
            ch.step(SP, "ctx", lambda e, turn, c=c, t=t: e.dma_start(t["ctx"][:], by_turn["ctx"][turn, c]),
                    [("before", "b_va"), ("before", "c_T1")], count="ctx")
            sequence_steps(ch, t, ps[:, 2 * c:2 * c + 2, :], k, dram)
            ch.open(nc, ctx)
            chains.append(ch)
            tiles.append(t)
        clear = ctx.enter_context(nc.semaphore("cleared"))
        unread = ctx.enter_context(nc.semaphore("unread"))

        parts = []
        for c, ch in enumerate(chains):
            steps = [s for s in ch.steps if s.engine != SP]
            spent = np.cumsum([s.cost for s in steps])
            cut = int(np.searchsorted(spent, spent[-1] * c / NCHAIN))
            parts.append(([(ch, s) for s in steps[:cut]], [(ch, s) for s in steps[cut:]]))

        def of(sequence, part):
            return [(ch, s, sequence) for ch, s in part]

        order_head = interleave([of(0, begin) for begin, _ in parts])
        order_turn = interleave([of(0, rest) + of(1, begin) for begin, rest in parts])
        order_tail = interleave([of(0, rest) for _, rest in parts])
        block = ctx.enter_context(nc.Block())

        def main(engine, name):
            for key, sem in setup.sems.items():
                engine.wait_ge(sem, setup.total[key] * (1 if key in (PE, DVE, ACTE, POOL) else 16))
            if name == POOL:
                for t in tiles:
                    for tile in ("kp", "vp", "mask_r", "fw3"):
                        engine.memset(t[tile][:], 0.0).then_inc(clear, 1)
                    engine.memset(t["va"][:], 1.0).then_inc(clear, 1)
            engine.wait_ge(clear, 5 * NCHAIN)
            if name == SP:
                for ch in chains:
                    for key in ("x_in", "mask_r", "mask_c", "ctx"):
                        engine.sem_inc(ch.sems[key], 16)
                with engine.Fori(0, TURNS) as turn:
                    for step in ("x_in", "mask_r", "mask_c", "ctx"):
                        run_queue(engine, [(ch, ch.by_name[step], 0) for ch in chains], turn, unread=unread)
                return
            for ch in chains:
                if name in ch.total:
                    engine.sem_inc(ch.sems[name], ch.total[name])
                if name == ACTE:
                    engine.sem_inc(ch.sems["store"], 16)
            run_queue(engine, order_head[name], 0, unread=unread)
            with engine.Fori(0, TURNS - 1) as turn:
                run_queue(engine, order_turn[name], turn, unread=unread)
            run_queue(engine, order_tail[name], TURNS - 1, unread=unread)
            if name == ACTE:
                for ch in chains:
                    engine.wait_ge(ch.sems["store"], 16 + 16 * TURNS)

        def program(name):
            def run(engine):
                run_queue(engine, [(setup, s, 0) for s in setup.steps if s.engine == name], 0, False)
                main(engine, name)
            return run

        for name in (SP, POOL, DVE, ACTE, PE):
            {SP: block.sync, POOL: block.gpsimd, DVE: block.vector, ACTE: block.scalar, PE: block.tensor}[name](program(name))


def shape_constants():
    p = np.arange(128)
    f = np.float32
    expand = np.zeros((4, 3, 8, 4, 128), f)
    for b in range(4):
        for r in range(128):
            expand[b, :, r // DH, b, r] = 1
    head_sum = np.zeros((128, KT, 32), f)
    for j in range(KT):
        head_sum[p, j, p // DH] = 1
    s = 32 * (p[:, None] // 32) + np.arange(32)[None, :]
    return {
        "ident": np.eye(128, dtype=f),
        "parity": np.stack([(p % 32 < 16), (p % 32 >= 16)], 1).astype(f),
        "head_sum": head_sum.reshape(128, KT * 32),
        "expand": expand.reshape(96, 4 * 128),
        "causal": np.where(p[None, :] > p[:, None], f(CAUSAL), f(0)),
        "rel": (p[None, None, :] - s[:, :, None]).astype(f).reshape(128, 32 * 128),
        "pos": np.tile(p.astype(f), (128, 1)),
        "pos7": np.tile(np.linspace(0.0, 1.0, WIN, dtype=f), (H, 1)),
        "diag16": np.tile(np.eye(H, dtype=f)[:, None, :], (1, WIN, 1)),
    }


def kernel(**inputs):
    import concourse.bacc as bacc
    from concourse.bass_utils import run_bass_kernel_spmd

    v = {name: np.asarray(a) for name, a in inputs.items()}
    w1 = v["L0_ffn_w1"]
    qkv_b = v["L1_attn_bqkv"]
    conv_w = v["L1_ffn_conv_w"].reshape(HT, 128, 3)

    def cols(a):
        return a.reshape(-1, 128).T

    laid = {
        "wqkv0T": np.concatenate([v["L0_attn_wq"].T, v["L0_attn_wk"].T, v["L0_attn_wv"].T], 1),
        "wo0T": v["L0_attn_wo"].T, "bo0": v["L0_attn_bo"],
        "cw1": v["L0_attn_cw1"].reshape(H, 32), "cb1": v["L0_attn_cb1"], "cw2": v["L0_attn_cw2"],
        "cb2": v["L0_attn_cb2"], "cw3": v["L0_attn_cw3"].reshape(H, 32), "cb3": v["L0_attn_cb3"],
        "wpT": v["L0_xattn_Wp"].T, "bp": v["L0_xattn_bp"],
        "slot_init": v["L0_ffn_slot_init"], "slot_scale": v["L0_ffn_slot_scale"],
        "w1aT": w1[:, :D].T, "w1bT": w1[:, D:].T, "b1f": cols(v["L0_ffn_b1"]), "w2fT": v["L0_ffn_w2"].T, "b2f": v["L0_ffn_b2"],
        "wihT": v["L0_ffn_gru_wih"].T, "whhT": v["L0_ffn_gru_whh"].T, "bih": v["L0_ffn_gru_bih"], "bhh": v["L0_ffn_gru_bhh"],
        "wvf": v["L0_ffn_wv"], "bvf": cols(v["L0_ffn_bv"]), "wofT": v["L0_ffn_wo"].T, "bof": v["L0_ffn_bo"], "tau": v["L0_ffn_tau"],
        "wqkv1": v["L1_attn_Wqkv"], "bq1": cols(qkv_b[:D]), "bk1": cols(qkv_b[D:2 * D]), "bv1": qkv_b[2 * D:],
        "wproj": v["L1_attn_Wproj"], "bproj": v["L1_attn_bproj"],
        "fw1": v["L1_attn_w1"].reshape(32, 1), "fb1": v["L1_attn_b1"].reshape(32, 1), "fw2": v["L1_attn_w2"],
        "fb2": v["L1_attn_b2"], "c_param": v["L1_attn_c_param"].reshape(1), "l_mult": v["L1_attn_L_multiplier"].reshape(1),
        "wqkvxT": np.concatenate([v["L1_xattn_Wq"].T, v["L1_xattn_Wk"].T, v["L1_xattn_Wv"].T], 1),
        "bqx": cols(v["L1_xattn_bq"]), "bkx": cols(v["L1_xattn_bk"]), "bvx": v["L1_xattn_bv"],
        "woxT": v["L1_xattn_Wo"].T, "box": v["L1_xattn_bo"],
        "w1t": v["L1_ffn_w1"].T, "w2t": v["L1_ffn_w2"].T,
        "conv_w": np.transpose(conv_w, (1, 0, 2)), "conv_b": v["L1_ffn_conv_b"].reshape(HT, 128).T,
        **shape_constants(),
    }
    nc = bacc.Bacc("TRN2", target_bir_lowering=False, num_devices=1)
    arrays, inp = {}, {}

    def given(name, a):
        arrays[name] = np.ascontiguousarray(a)
        return nc.dram_tensor(name, arrays[name].shape, F32, kind="ExternalInput").ap()

    for name, a in laid.items():
        inp[name] = given("in_" + name, a)
    x, c, m = given("in_x", v["x"]), given("in_ctx", v["ctx_1024"]), given("in_mask", v["mask_BxS2_fk1"])
    out = nc.dram_tensor("out", (NSEQ, T, D), F32, kind="ExternalOutput").ap()
    decoder(nc, inp, x, c, m, out)
    return run_bass_kernel_spmd(nc, [arrays], core_ids=[0]).results[0]["out"]
```
